# Optimizing a Trainium2 kernel written in Bass

```python
import numpy as np
import jax
import jax.numpy as jnp

def _softmax(x, axis=-1):
    return jax.nn.softmax(x, axis=axis)
def _gelu(x):
    return jax.nn.gelu(x, approximate=True)
def _silu(x):
    return jax.nn.silu(x)
def _sigmoid(x):
    return jax.nn.sigmoid(x)
def _layernorm(x, axis=-1, eps=1e-5):
    m = jnp.mean(x, axis=axis, keepdims=True)
    v = jnp.var(x, axis=axis, keepdims=True)
    return (x - m) / jnp.sqrt(v + eps)
def _scatter_add(tgt, idx, src, axis=0):
    return tgt.at[idx].add(src)
def _segment_sum(src, seg, n):
    return jax.ops.segment_sum(src, seg, n)

kernel_name = 'mk_conv_preact_d2_conv_nchw128_fa776f'

def setup_inputs(seed: int = 0):
    np.random.seed(seed)
    _w = jnp.asarray
    def _rec_inputs():
        import jax
        import jax.numpy as jnp
        _gk = jax.random.key(seed)
        x = -0.0003929 + 0.9999 * jax.random.normal(jax.random.fold_in(_gk, 1), (8, 128, 128, 128), jnp.float32)
        return x
    x = _rec_inputs()
    def _L0_conv_setup():
        import jax, jax.numpy as jnp
        import numpy as np
        HEADS = 4
        DIM_HEAD = 32
        DIM = 128
        HIDDEN = HEADS * DIM_HEAD
        key = jax.random.key(seed)
        k1, k2, k3, k4 = jax.random.split(key, 4)
        B, C, H, W = (8, DIM, 128, 128)
        x = jax.random.normal(k1, (B, C, H, W), dtype=jnp.float32)
        w_qkv = jax.random.normal(k2, (3 * HIDDEN, DIM), dtype=jnp.float32) * (1.0 / np.sqrt(DIM))
        w_out = jax.random.normal(k3, (DIM, HIDDEN), dtype=jnp.float32) * (1.0 / np.sqrt(HIDDEN))
        b_out = jax.random.normal(k4, (DIM,), dtype=jnp.float32) * 0.01
        return {'x': x, 'w_qkv': w_qkv, 'w_out': w_out, 'b_out': b_out}
    _L0_conv_all = _L0_conv_setup()
    _L0_conv_in = {k: v for k, v in _L0_conv_all.items() if k in ('w_qkv', 'w_out', 'b_out', )}
    del _L0_conv_all

    def _L1_conv_setup():
        import jax, jax.numpy as jnp
        import numpy as np
        K = 3
        OUT = 128
        PAD = K // 2
        key = jax.random.key(seed)
        k1, k2 = jax.random.split(key)
        x = jax.random.normal(k1, (32, 128, 56, 56), dtype=jnp.float32)
        weight = jax.random.normal(k2, (K * K * OUT, 128), dtype=jnp.float32) * 0.05
        return {'x': x, 'weight': weight}
    _L1_conv_all = _L1_conv_setup()
    _L1_conv_in = {k: v for k, v in _L1_conv_all.items() if k in ('weight', )}
    del _L1_conv_all

    return {
        "x": x,
        "L0_conv_w_qkv": _L0_conv_in["w_qkv"],
        "L0_conv_w_out": _L0_conv_in["w_out"],
        "L0_conv_b_out": _L0_conv_in["b_out"],
        "L1_conv_weight": _L1_conv_in["weight"],
    }

def reference(x, L0_conv_w_qkv, L0_conv_w_out, L0_conv_b_out, L1_conv_weight):
    import jax
    import jax.numpy as jnp
    def _L0_conv_ref(x, w_qkv, w_out, b_out):
        import jax, jax.numpy as jnp
        import numpy as np
        HEADS = 4
        DIM_HEAD = 32
        DIM = 128
        HIDDEN = HEADS * DIM_HEAD
        b, c, h, w = x.shape
        n = h * w
        qkv = jnp.einsum('bchw,oc->bohw', x, w_qkv)
        qkv = qkv.reshape(b, 3, HEADS, DIM_HEAD, n)
        q, k, v = (qkv[:, 0], qkv[:, 1], qkv[:, 2])
        k = jax.nn.softmax(k, axis=-1)
        context = jnp.einsum('bhdn,bhen->bhde', k, v)
        out = jnp.einsum('bhde,bhdn->bhen', context, q)
        out = out.reshape(b, HIDDEN, h, w)
        y = jnp.einsum('bchw,oc->bohw', out, w_out) + b_out[None, :, None, None]
        return y

    def _L1_conv_ref(x, weight):
        import jax, jax.numpy as jnp
        import numpy as np
        K = 3
        OUT = 128
        PAD = K // 2
        in_ch = x.shape[1]
        w = weight.reshape(K, K, OUT, in_ch).transpose(2, 3, 0, 1)
        return jax.lax.conv_general_dilated(x, w, window_strides=(1, 1), padding=((PAD, PAD), (PAD, PAD)), dimension_numbers=('NCHW', 'OIHW', 'NCHW'))

    def _gn(v, G=32, eps=1e-5):
        B_, C_, H_, W_ = v.shape
        g = v.reshape(B_, G, C_ // G, H_, W_)
        m = jnp.mean(g, axis=(2, 3, 4), keepdims=True)
        s = jnp.var(g, axis=(2, 3, 4), keepdims=True)
        return ((g - m) / jnp.sqrt(s + eps)).reshape(v.shape)

    def _ln_c(v, eps=1e-6):
        m = jnp.mean(v, axis=1, keepdims=True)
        s = jnp.var(v, axis=1, keepdims=True)
        return (v - m) / jnp.sqrt(s + eps)

    def _ln_t(v, eps=1e-5):
        m = jnp.mean(v, axis=-1, keepdims=True)
        s = jnp.var(v, axis=-1, keepdims=True)
        return (v - m) / jnp.sqrt(s + eps)

    def _to_tokens(v):
        B_, C_, H_, W_ = v.shape
        return v.reshape(B_, C_, H_ * W_).transpose(0, 2, 1)
    def _from_tokens(t, like):
        B_, C_, H_, W_ = like.shape
        return t.transpose(0, 2, 1).reshape(B_, C_, H_, W_)

    x = x + _L0_conv_ref(_gn(x), L0_conv_w_qkv, L0_conv_w_out, L0_conv_b_out)
    x = x + _L1_conv_ref(_gn(x), L1_conv_weight)
    return x


_drawn_inputs = setup_inputs


def setup_inputs(seed=0):
    import zlib

    import numpy as np

    out = dict(_drawn_inputs(seed))
    spreads = {}
    factors = {'L0_conv_b_out': 6.295}
    for name, (base, spread) in spreads.items():
        noise = np.random.default_rng([zlib.crc32(name.encode()), seed]).standard_normal(out[name].shape)
        drawn = base * np.exp(spread * noise) if base else spread * noise
        out[name] = jnp.asarray(drawn.astype(out[name].dtype))
    for name, factor in factors.items():
        out[name] = (out[name] * factor).astype(out[name].dtype)
    return out
```

```python
from contextlib import ExitStack

import numpy as np
import concourse.bass as bass
import concourse.mybir as mybir

IMAGES, CH, HEIGHT, WIDTH = 8, 128, 128, 128
PIXELS = HEIGHT * WIDTH
GROUPS = 32
HEADS = 4
TAPS = 9
EPS = 1e-5

CHUNK = 512
ROWS = CHUNK // WIDTH
TILES = PIXELS // CHUNK
SUB = CHUNK // 128
LOADS = 8
PER_LOAD = TILES // LOADS
STORES = TILES // 2
MACROS = TILES // 4
RING = 4 * ROWS + 2
PADDED = WIDTH + 2
ONES = 2
GRAM = ONES + 2 * CH
HUGE = 3.0e38
CENTRE = TAPS // 2
W_PIECES = [[0, 1, 2, 3], [5, 6, 7, 8], [CENTRE]]
CHAIN = 4


def attention_work(macro, tile):
    if macro == 0:
        return [("stats", j) for j in range(4 * tile, 4 * tile + 4)]
    if macro == 1:
        return [[("stats", j) for j in range(16, 24)],
                [("stats", j) for j in range(24, 32)] + [("gather",)],
                [("mean",), ("variance",)],
                [("first",)]][tile]
    if macro == 6:
        return [[("chain", n) for n in range(CHAIN)]] [tile] if tile == 0 else \
               [("project", j) for j in range(5 * tile - 5, 5 * tile)]
    if macro == 7:
        return [[("project", j) for j in range(15, 21)],
                [("project", j) for j in range(21, 27)],
                [("project", j) for j in range(27, 32)],
                [("mean",), ("variance",)]][tile]
    return None


ATTEND = range(2, 6)


def build(nc, x, w_key, w_value, w_query, w_out, b_out, w_conv, identity, group_mean, head_mask, out):
    f32, f32r = mybir.dt.float32, mybir.dt.float32r
    ALU, ACT = mybir.AluOpType, mybir.ActivationFunctionType
    ctx = ExitStack()
    with ctx:
        def sb(name, shape, dt=f32):
            return ctx.enter_context(nc.sbuf_tensor(name, shape, dt))

        def ps(name, shape):
            return ctx.enter_context(nc.psum_tensor(name, shape, f32))

        def sem(name):
            return ctx.enter_context(nc.semaphore(name))

        x_img = sb("x_img", [CH, PIXELS])
        x1_img = sb("x1_img", [CH, PIXELS])
        ring_hi = sb("ring_hi", [CH, RING, PADDED], f32r)
        ring_lo = sb("ring_lo", [CH, RING, PADDED], f32r)
        wc_raw = sb("wc_raw", [CH, TAPS * CH])
        wc_mid = sb("wc_mid", [CH, CH])
        wc_hi = sb("wc_hi", [CH, TAPS * CH], f32r)
        wc_lo = sb("wc_lo", [CH, TAPS * CH], f32r)
        out_stage = sb("out_stage", [CH, 2, 2 * CHUNK])
        xc = sb("xc", [CH, 2, CHUNK])
        xs_hi = sb("xs_hi", [CH, 2, CHUNK], f32r)
        xs_lo = sb("xs_lo", [CH, 2, CHUNK], f32r)
        e_chunk = sb("e_chunk", [CH, 2, CHUNK])
        et_hi = sb("et_hi", [128, SUB, CH], f32r)
        et_lo = sb("et_lo", [128, SUB, CH], f32r)
        xt = sb("xt", [128, SUB, GRAM], f32r)
        gram = sb("gram", [CH, GRAM])
        neg_max = sb("neg_max", [CH, 4])
        alpha = sb("alpha", [CH, 4])
        wk_raw = sb("wk_raw", [CH, CH])
        wv_sb = sb("wv_sb", [CH, CH])
        wq_sb = sb("wq_sb", [CH, CH])
        wo_sb = sb("wo_sb", [CH, CH])
        ident = sb("ident", [CH, CH])
        gmat = sb("gmat", [CH, CH])
        mask = sb("mask", [CH, CH])
        wk_tmp = sb("wk_tmp", [CH, CH])
        wk_hi = sb("wk_hi", [CH, CH], f32r)
        wk_lo = sb("wk_lo", [CH, CH], f32r)
        chain_sb = sb("chain_sb", [CH, CH])
        a_full = sb("a_full", [CH, CH])
        a_hi = sb("a_hi", [CH, CH], f32r)
        a_lo = sb("a_lo", [CH, CH], f32r)
        stats = sb("stats", [CH, TILES * 6])
        moments = sb("moments", [CH, 2, 2])
        shift = sb("shift", [CH, 2])
        dev = sb("dev", [CH, 2])
        var_in = sb("var_in", [CH, 2])
        var_eps = sb("var_eps", [CH, 2])
        rstd = sb("rstd", [CH, 2])
        minus_half = sb("minus_half", [CH, 1])
        b_sb = sb("b_sb", [CH, 1])
        x1_bias = sb("x1_bias", [CH, 1])
        out_bias = sb("out_bias", [CH, 1])
        denom_inv = sb("denom_inv", [CH, 1])

        conv_ps = ps("conv_ps", [CH, 2, CHUNK])
        proj_ps = ps("proj_ps", [CH, 2, CHUNK])
        xt_ps = ps("xt_ps", [128, CHUNK])
        et_ps = ps("et_ps", [128, CHUNK])
        gram_ps = ps("gram_ps", [CH, CHUNK])
        small_ps = ps("small_ps", [CH, CHUNK])
        mean_ps, var_ps, mat_ps = small_ps[:, 0:1], small_ps[:, 4:5], small_ps[:, 128:128 + CH]

        weights_loaded = sem("weights_loaded")
        constants_set = sem("constants_set")
        x_loaded = [sem(f"x_loaded{g}") for g in range(LOADS)]
        stage_free = [sem(f"stage_free{s}") for s in range(2)]
        moments_ready = sem("moments_ready")
        mean_done = sem("mean_done")
        shift_ready = sem("shift_ready")
        var_in_ready = sem("var_in_ready")
        var_done = sem("var_done")
        var_eps_ready = sem("var_eps_ready")
        rstd_ready = sem("rstd_ready")
        start_set = sem("start_set")
        wk_ready = sem("wk_ready")
        xc_ready = sem("xc_ready")
        key_hi_ready = sem("key_hi_ready")
        key_lo_ready = sem("key_lo_ready")
        key_done = sem("key_done")
        max_ready = sem("max_ready")
        exp_ready = sem("exp_ready")
        alpha_ready = sem("alpha_ready")
        xt_done = sem("xt_done")
        et_done = sem("et_done")
        xt_hi_ready = sem("xt_hi_ready")
        et_hi_ready = sem("et_hi_ready")
        xt_lo_ready = sem("xt_lo_ready")
        et_lo_ready = sem("et_lo_ready")
        gram_done = sem("gram_done")
        gram_added = sem("gram_added")
        chain_in = sem("chain_in")
        chain_out = sem("chain_out")
        a_ready = sem("a_ready")
        proj_hi_ready = sem("proj_hi_ready")
        proj_lo_ready = sem("proj_lo_ready")
        proj_done = sem("proj_done")
        x1_ready = sem("x1_ready")
        ring_hi_ready = sem("ring_hi_ready")
        ring_lo_ready = sem("ring_lo_ready")
        wc_mid_ready = sem("wc_mid_ready")
        wc_hi_ready = sem("wc_hi_ready")
        wc_lo_ready = sem("wc_lo_ready")
        conv_done = sem("conv_done")
        conv_taken = sem("conv_taken")
        halo_zeroed = sem("halo_zeroed")
        out_bias_ready = sem("out_bias_ready")
        dve_settled = sem("dve_settled")
        DVE_STEPS = 11

        def x_chunk(j):
            return x_img[:, bass.ds(j * CHUNK, CHUNK)]

        def x1_chunk(j):
            return x1_img[:, bass.ds(j * CHUNK, CHUNK)]

        def rows(ap):
            return ap.rearrange("c (r w) -> c r w", w=WIDTH)

        def blocks(ap):
            return ap.rearrange("n (s c) -> n s c", c=CH)

        def image_steps(engine, macro_step, transition):
            def step(q, conv, attend):
                def macro(i):
                    macro_step(i, q, conv, attend)
                if attend:
                    for i in range(ATTEND.start):
                        macro(i)
                    with engine.Fori(ATTEND.start, ATTEND.stop - 1) as i:
                        macro(i)
                    for i in range(ATTEND.stop - 1, MACROS):
                        macro(i)
                else:
                    with engine.Fori(0, MACROS - 1) as i:
                        macro(i)
                    macro(MACROS - 1)
                transition(q, conv, attend)
            step(0, False, True)
            with engine.Fori(1, IMAGES) as q:
                step(q, True, True)
            step(IMAGES, True, False)

        def work_of(i, tile, attend):
            if not attend:
                return []
            if not isinstance(i, int) or i in ATTEND:
                j = (i - ATTEND.start) * 8 + 2 * tile
                return [("attend", j, 2 * tile), ("attend", j + 1, 2 * tile + 1)]
            return attention_work(i, tile)

        def more(j, ahead):
            return not isinstance(j, int) or j + ahead < TILES

        block = ctx.enter_context(nc.Block())

        @block.sync
        def _(sp):
            def load(q, g):
                sp.dma_start(x_img[:, g * PER_LOAD * CHUNK:(g + 1) * PER_LOAD * CHUNK],
                             x[q, :, g * PER_LOAD * CHUNK:(g + 1) * PER_LOAD * CHUNK]).then_inc(x_loaded[g], 16)

            def reload(q, g):
                sp.wait_ge(proj_lo_ready, TILES * (q - 1) + PER_LOAD * (g + 1))
                load(q, g)

            def store(p, u, slot):
                sp.wait_ge(conv_taken, TILES * p + 2 * u + 2)
                sp.dma_start(out[p, :, bass.ds(u * 2 * CHUNK, 2 * CHUNK)], out_stage[:, slot, :]).then_inc(stage_free[slot], 16)

            def early_stores(p, count):
                with sp.Fori(0, count // 2) as v:
                    store(p, 2 * v, 0)
                    store(p, 2 * v + 1, 1)

            for g in range(LOADS):
                load(0, g)
            for g in range(LOADS):
                reload(1, g)

            def late(p, reloading):
                q = p + 2
                for what, n in [("r", 0), ("s", 12), ("r", 1), ("r", 2), ("r", 3), ("s", 13), ("r", 4), ("r", 5),
                                ("r", 6), ("s", 14), ("r", 7), ("s", 15)]:
                    if what == "s":
                        store(p, n, n % 2)
                    elif reloading:
                        reload(q, n)
            with sp.Fori(0, IMAGES - 2) as p:
                early_stores(p, 12)
                late(p, True)
            for p in (IMAGES - 2, IMAGES - 1):
                early_stores(p, 12)
                late(p, False)
            for s in range(2):
                sp.wait_ge(stage_free[s], 16 * (IMAGES * STORES // 2 + 1))

        @block.tensor
        def _(pe):
            def three(ps_out, w_hi, w_lo, m_hi, m_lo, start, stop):
                pe.matmul(ps_out, w_hi, m_hi, start=start, stop=False)
                pe.matmul(ps_out, w_hi, m_lo, start=False, stop=False)
                return pe.matmul(ps_out, w_lo, m_hi, start=False, stop=stop)

            def conv_taps(p, i, tile, part, parts, attend):
                taps = [tap for piece in W_PIECES for tap in piece]
                t = 4 * i + tile
                first_tile = t == 0 if isinstance(i, int) else tile == 0 and not attend
                if part == 0:
                    last_tile = isinstance(i, int) and t == TILES - 1
                    pe.wait_ge(ring_lo_ready, TILES * p + t + (1 if last_tile else 2))
                    if last_tile:
                        pe.wait_ge(halo_zeroed, p + 1)
                    if not isinstance(i, int) or t > 1:
                        pe.wait_ge(conv_taken, TILES * p + t - 1)
                    elif t == 1:
                        pe.wait_ge(out_bias_ready, p + 1)
                lo, hi = TAPS * part // parts, TAPS * (part + 1) // parts
                for n in range(lo, hi):
                    tap = taps[n]
                    dy, dx = tap // 3, tap % 3
                    if first_tile:
                        for k, piece in enumerate(W_PIECES):
                            if piece[0] == tap:
                                pe.wait_ge(wc_lo_ready, len(W_PIECES) * p + k + 1)
                    w = slice(tap * CH, (tap + 1) * CH)
                    window = (slice(None), slice(ROWS * tile + dy, ROWS * tile + dy + ROWS), slice(dx, dx + WIDTH))
                    last = three(rows(conv_ps[:, tile % 2, :]), wc_hi[:, w], wc_lo[:, w],
                                 ring_hi[window], ring_lo[window], n == 0, n == TAPS - 1)
                if part == parts - 1:
                    last.then_inc(conv_done, 1)

            def key(q, j, slot):
                pe.wait_ge(key_lo_ready, TILES * q + j + 1)
                three(proj_ps[:, slot, :], wk_hi[:, :], wk_lo[:, :], xs_hi[:, slot, :], xs_lo[:, slot, :],
                      True, True).then_inc(key_done, 1)

            def turn(q, j, slot):
                pe.wait_ge(xc_ready, TILES * q + j + 1)
                for s in range(SUB):
                    last = pe.transpose(xt_ps[:, s * 128:(s + 1) * 128], xc[:, slot, s * 128:(s + 1) * 128], ident[:, :])
                last.then_inc(xt_done, 1)
                pe.wait_ge(exp_ready, TILES * q + j + 1)
                for s in range(SUB):
                    last = pe.transpose(et_ps[:, s * 128:(s + 1) * 128], e_chunk[:, slot, s * 128:(s + 1) * 128], ident[:, :])
                last.then_inc(et_done, 1)

            def gram_product(q, j):
                pe.wait_ge(xt_lo_ready, TILES * q + j + 1)
                pe.wait_ge(et_lo_ready, TILES * q + j + 1)
                pe.wait_ge(gram_added, (TILES + 1) * q + j + 1)
                for s in range(SUB):
                    pe.matmul(gram_ps[:, 0:GRAM], et_hi[:, s, :], xt[:, s, :], start=(s == 0), stop=False)
                    last = pe.matmul(gram_ps[:, 0:ONES + CH], et_lo[:, s, :], xt[:, s, 0:ONES + CH],
                                     start=False, stop=(s == SUB - 1))
                last.then_inc(gram_done, 1)

            def chain(q, n):
                pe.wait_ge(chain_in, CHAIN * q + n + 1)
                if n == 0:
                    last = pe.transpose(mat_ps, gram[:, ONES:ONES + CH], ident[:, :])
                elif n == 1:
                    last = pe.matmul(mat_ps, wv_sb[:, :], chain_sb[:, :], start=True, stop=True)
                elif n == 2:
                    last = pe.matmul(mat_ps, chain_sb[:, :], wo_sb[:, :], start=True, stop=True)
                else:
                    last = pe.matmul(mat_ps, wq_sb[:, :], chain_sb[:, :], start=True, stop=True)
                last.then_inc(chain_out, 1)

            def project(q, j):
                if j == 0:
                    pe.wait_ge(a_ready, q + 1)
                pe.wait_ge(proj_lo_ready, TILES * q + j + 1)
                if j >= 2:
                    pe.wait_ge(x1_ready, TILES * q + j - 1)
                three(proj_ps[:, j % 2, :], a_hi[:, :], a_lo[:, :], xs_hi[:, j % 2, :], xs_lo[:, j % 2, :],
                      True, True).then_inc(proj_done, 1)

            def macro_step(i, q, conv, attend):
                for tile in range(4):
                    work = [w for w in work_of(i, tile, attend) if w[0] not in ("stats", "gather")]
                    norm = 0 if isinstance(i, int) and i < MACROS - 1 else 1
                    parts = 3 if work and work[0][0] == "mean" else max(1, len(work))
                    for part in range(parts):
                        w = work[part] if part < len(work) else ("none",)
                        if w[0] == "attend":
                            j, slot = w[1], w[2] % 2
                            if more(j, 1):
                                key(q, j + 1, 1 - slot)
                            turn(q, j, slot)
                        elif w[0] == "chain":
                            chain(q, w[1])
                        elif w[0] == "project":
                            project(q, w[1])
                        if conv:
                            conv_taps(q - 1, i, tile, part, parts, attend)
                        if w[0] == "attend":
                            gram_product(q, w[1])
                        elif w[0] == "mean":
                            pe.wait_ge(moments_ready, 2 * q + norm + 1)
                            pe.matmul(mean_ps, gmat[:, :], moments[:, norm, 0:1], start=True, stop=True).then_inc(mean_done, 1)
                        elif w[0] == "variance":
                            pe.wait_ge(var_in_ready, 2 * q + norm + 1)
                            pe.matmul(var_ps, gmat[:, :], var_in[:, norm:norm + 1], start=True, stop=True).then_inc(var_done, 1)
                        elif w[0] == "first":
                            pe.wait_ge(wk_ready, q + 1)
                            key(q, 0, 0)

            pe.wait_ge(weights_loaded, 16 * 9)
            pe.wait_ge(constants_set, 4)
            image_steps(pe, macro_step, lambda q, conv, attend: None)

        @block.scalar
        def _(act):
            for dst, src in ((ident, identity), (gmat, group_mean), (mask, head_mask), (wk_raw, w_key), (wv_sb, w_value),
                             (wq_sb, w_query), (wo_sb, w_out), (b_sb, b_out), (wc_raw, w_conv)):
                act.dma_start(dst[:, :], src).then_inc(weights_loaded, 16)

            for slot in range(2):
                act.sem_inc(stage_free[slot], 16)

            def exp_chunk(q, j, k):
                act.wait_ge(max_ready, TILES * q + j + 1)
                act.activation(e_chunk[:, k % 2, :], proj_ps[:, k % 2, :], ACT.Exp, bias=neg_max[:, k % 4:k % 4 + 1],
                               scale=-1.0).then_inc(exp_ready, 1)
                act.activation(alpha[:, k % 4:k % 4 + 1], neg_max[:, (k - 1) % 4:(k - 1) % 4 + 1], ACT.Exp,
                               bias=neg_max[:, k % 4:k % 4 + 1], scale=-1.0).then_inc(alpha_ready, 1)

            def key_hi(q, j, slot):
                act.wait_ge(xc_ready, TILES * q + j + 1)
                if not (isinstance(j, int) and j < 2):
                    act.wait_ge(key_done, TILES * q + j - 1)
                act.activation(xs_hi[:, slot, :], xc[:, slot, :], ACT.Identity).then_inc(key_hi_ready, 1)

            def proj_hi(q, j):
                if j >= 2:
                    act.wait_ge(proj_done, TILES * q + j - 1)
                act.activation(xs_hi[:, j % 2, :], x_chunk(j), ACT.Identity, bias=shift[:, 0:1]).then_inc(proj_hi_ready, 1)

            def take_x1(q, conv, j):
                act.wait_ge(proj_done, TILES * q + j + 1)
                if conv:
                    act.wait_ge(ring_lo_ready, TILES * (q - 1) + j + 1)
                act.activation(x1_chunk(j), proj_ps[:, j % 2, :], ACT.Identity, bias=x1_bias[:, 0:1]).then_inc(x1_ready, 1)

            def split_rows(p, t, tile, top, bottom, ring_fresh=False):
                if not ring_fresh and (not isinstance(t, int) or t != 2):
                    act.wait_ge(conv_done, TILES * p + t - 2)
                src = rows(x1_chunk(t))
                r0 = 1 + ROWS * tile
                if top:
                    act.activation(ring_hi[:, 0, 1:1 + WIDTH], src[:, ROWS - 1, :], ACT.Identity, bias=shift[:, 1:2])
                if bottom:
                    act.activation(ring_hi[:, RING - 1, 1:1 + WIDTH], src[:, 0, :], ACT.Identity, bias=shift[:, 1:2])
                act.activation(ring_hi[:, r0:r0 + ROWS, 1:1 + WIDTH], src, ACT.Identity,
                               bias=shift[:, 1:2]).then_inc(ring_hi_ready, 1)

            def take_conv(p, i, tile):
                t = 4 * i + tile
                slot = (tile // 2) % 2
                act.wait_ge(conv_done, TILES * p + t + 1)
                if tile % 2 == 0:
                    act.wait_ge(stage_free[slot], 16 * (MACROS * p + i + 1))
                act.activation(out_stage[:, slot, (tile % 2) * CHUNK:(tile % 2 + 1) * CHUNK], conv_ps[:, tile % 2, :],
                               ACT.Identity, bias=out_bias[:, 0:1]).then_inc(conv_taken, 1)

            def macro_step(i, q, conv, attend):
                for tile in range(4):
                    work = work_of(i, tile, attend)
                    if conv:
                        if tile > 0:
                            take_conv(q - 1, i, tile - 1)
                        elif not isinstance(i, int) or i > 0:
                            if attend:
                                take_conv(q - 1, i - 1, 3)
                        last_round = isinstance(i, int) and i == MACROS - 1
                        if not (last_round and tile >= 2):
                            ahead = (tile + 2) % 4
                            split_rows(q - 1, 4 * i + tile + 2, ahead, ahead == 3 and not last_round, ahead == 0)
                    for w in work:
                        if w[0] == "attend":
                            j, k = w[1], w[2]
                            act.wait_ge(xt_done, TILES * q + j + 1)
                            act.activation(xt[:, :, ONES:ONES + CH], blocks(xt_ps[:, :]), ACT.Identity).then_inc(xt_hi_ready, 1)
                            act.wait_ge(et_done, TILES * q + j + 1)
                            act.activation(et_hi[:, :, :], blocks(et_ps[:, :]), ACT.Identity).then_inc(et_hi_ready, 1)
                            if more(j, 1):
                                exp_chunk(q, j + 1, k + 1)
                            if more(j, 2):
                                key_hi(q, j + 2, k % 2)
                        elif w[0] == "first":
                            key_hi(q, 0, 0)
                            key_hi(q, 1, 1)
                            exp_chunk(q, 0, 0)
                        elif w == ("chain", CHAIN - 1):
                            proj_hi(q, 0)
                            proj_hi(q, 1)
                        elif w[0] == "project":
                            take_x1(q, conv, w[1])
                            if more(w[1], 2):
                                proj_hi(q, w[1] + 2)
                    if conv and not attend and not isinstance(i, int) and tile == 3:
                        take_conv(q - 1, i, 3)

            def transition(q, conv, attend):
                if attend:
                    act.wait_ge(shift_ready, 2 * q + 2)
                    split_rows(q, 0, 0, False, False, ring_fresh=not conv)
                    split_rows(q, 1, 1, False, False, ring_fresh=not conv)
                    act.wait_ge(rstd_ready, 2 * q + 2)
                    if conv:
                        act.wait_ge(conv_done, TILES * q)
                    for k, piece in enumerate(W_PIECES):
                        w = slice(piece[0] * CH, (piece[-1] + 1) * CH)
                        if piece == [CENTRE]:
                            act.wait_ge(wc_mid_ready, q + 1)
                            act.activation(wc_hi[:, w], wc_mid[:, :], ACT.Identity).then_inc(wc_hi_ready, 1)
                        else:
                            act.activation(wc_hi[:, w], wc_raw[:, w], ACT.Identity, scale=rstd[:, 1:2]).then_inc(wc_hi_ready, 1)
                if conv:
                    take_conv(q - 1, MACROS - 1, 3)
                if attend:
                    act.wait_ge(out_bias_ready, q + 1)

            act.wait_ge(constants_set, 4)
            act.wait_ge(weights_loaded, 16 * 9)
            image_steps(act, macro_step, transition)

        @block.vector
        def _(dve):
            steps = [0]

            def settle(q, instruction):
                steps[0] += 1
                instruction.then_inc(dve_settled, 1)
                dve.wait_ge(dve_settled, DVE_STEPS * q + steps[0])

            def group_norm(q, norm, stage):
                n = 2 * q + norm + 1
                if stage == "gather":
                    if norm == 0:
                        dve.memset(neg_max[:, 3:4], HUGE).then_inc(start_set, 1)
                    else:
                        dve.memset(gram[:, :], 0.0).then_inc(gram_added, 1)
                    dve.bn_aggr(moments[:, norm, :], stats[:, :]).then_inc(moments_ready, 1)
                elif stage == "mean":
                    dve.wait_ge(mean_done, n)
                    dve.wait_ge(moments_ready, n)
                    dve.tensor_scalar(shift[:, norm:norm + 1], mean_ps, -1.0, None, ALU.mult).then_inc(shift_ready, 1)
                    settle(q, dve.tensor_tensor(dev[:, norm:norm + 1], moments[:, norm, 0:1], mean_ps, ALU.subtract))
                    dve.scalar_tensor_tensor(out=var_in[:, norm:norm + 1], in0=dev[:, norm:norm + 1],
                                             scalar=dev[:, norm:norm + 1], in1=moments[:, norm, 1:2],
                                             op0=ALU.mult, op1=ALU.add).then_inc(var_in_ready, 1)
                else:
                    dve.wait_ge(var_done, n)
                    dve.tensor_scalar(var_eps[:, norm:norm + 1], var_ps, EPS, None, ALU.add).then_inc(var_eps_ready, 1)

            def centre(q, j, slot):
                if not (isinstance(j, int) and j < 2):
                    dve.wait_ge(xt_done, TILES * q + j - 1)
                    dve.wait_ge(key_lo_ready, TILES * q + j - 1)
                dve.tensor_scalar(xc[:, slot, :], x_chunk(j), shift[:, 0:1], None, ALU.add).then_inc(xc_ready, 1)

            def running_max(q, j, k):
                dve.wait_ge(key_done, TILES * q + j + 1)
                if not (isinstance(j, int) and j == 0):
                    dve.wait_ge(max_ready, TILES * q + j)
                dve.tensor_scalar(e_chunk[:, k % 2, :], proj_ps[:, k % 2, :], 1.0, neg_max[:, (k - 1) % 4:(k - 1) % 4 + 1],
                                  ALU.mult, ALU.min, accum_out=neg_max[:, k % 4:k % 4 + 1]).then_inc(max_ready, 1)

            def add_gram(q, j, k):
                dve.wait_ge(gram_done, TILES * q + j + 1)
                dve.wait_ge(alpha_ready, TILES * q + j + 1)
                dve.wait_ge(gram_added, (TILES + 1) * q + j + 1)
                dve.scalar_tensor_tensor(out=gram[:, :], in0=gram[:, :], scalar=alpha[:, k % 4:k % 4 + 1],
                                         in1=gram_ps[:, 0:GRAM], op0=ALU.mult, op1=ALU.add).then_inc(gram_added, 1)

            def proj_lo(q, j):
                dve.wait_ge(proj_hi_ready, TILES * q + j + 1)
                dve.scalar_tensor_tensor(out=xs_lo[:, j % 2, :], in0=x_chunk(j), scalar=shift[:, 0:1],
                                         in1=xs_hi[:, j % 2, :].bitcast(f32), op0=ALU.add,
                                         op1=ALU.subtract).then_inc(proj_lo_ready, 1)

            def split_rows(p, t, tile, top, bottom):
                dve.wait_ge(ring_hi_ready, TILES * p + t + 1)
                src = rows(x1_chunk(t))
                r0 = 1 + ROWS * tile
                for slot, row in ((0, ROWS - 1),) * top + ((RING - 1, 0),) * bottom:
                    dve.scalar_tensor_tensor(out=ring_lo[:, slot, 1:1 + WIDTH], in0=src[:, row, :], scalar=shift[:, 1:2],
                                             in1=ring_hi[:, slot, 1:1 + WIDTH].bitcast(f32), op0=ALU.add, op1=ALU.subtract)
                dve.scalar_tensor_tensor(out=ring_lo[:, r0:r0 + ROWS, 1:1 + WIDTH], in0=src, scalar=shift[:, 1:2],
                                         in1=ring_hi[:, r0:r0 + ROWS, 1:1 + WIDTH].bitcast(f32), op0=ALU.add,
                                         op1=ALU.subtract).then_inc(ring_lo_ready, 1)

            def start_attention(q):
                centre(q, 0, 0)
                centre(q, 1, 1)
                dve.tensor_tensor(x1_bias[:, :], b_sb[:, :], shift[:, 0:1], ALU.subtract)
                dve.wait_ge(rstd_ready, 2 * q + 1)
                settle(q, dve.tensor_scalar(wk_tmp[:, :], wk_raw[:, :], rstd[:, 0:1], -1.0, ALU.mult, ALU.mult))
                settle(q, dve.tensor_copy(wk_hi[:, :], wk_tmp[:, :]))
                dve.tensor_tensor(wk_lo[:, :], wk_tmp[:, :], wk_hi[:, :].bitcast(f32), ALU.subtract).then_inc(wk_ready, 1)
                dve.wait_ge(start_set, q + 1)
                running_max(q, 0, 0)

            def chain(q, n):
                if n == 0:
                    dve.wait_ge(gram_added, (TILES + 1) * (q + 1))
                    settle(q, dve.reciprocal(denom_inv[:, :], gram[:, 0:1]))
                    settle(q, dve.tensor_tensor(gram[:, ONES:ONES + CH], gram[:, ONES:ONES + CH],
                                                gram[:, ONES + CH:GRAM], ALU.add))
                    dve.tensor_scalar(gram[:, ONES:ONES + CH], gram[:, ONES:ONES + CH], denom_inv[:, 0:1], None,
                                      ALU.mult).then_inc(chain_in, 1)
                    dve.wait_ge(chain_out, CHAIN * q + 1)
                    dve.tensor_scalar(chain_sb[:, :], mat_ps, rstd[:, 0:1], None, ALU.mult).then_inc(chain_in, 1)
                elif n == 1:
                    dve.wait_ge(chain_out, CHAIN * q + 2)
                    dve.tensor_tensor(chain_sb[:, :], mat_ps, mask[:, :], ALU.mult).then_inc(chain_in, 1)
                elif n == 2:
                    dve.wait_ge(chain_out, CHAIN * q + 3)
                    dve.tensor_copy(chain_sb[:, :], mat_ps).then_inc(chain_in, 1)
                else:
                    dve.wait_ge(chain_out, CHAIN * q + 4)
                    settle(q, dve.scalar_tensor_tensor(out=a_full[:, :], in0=mat_ps, scalar=rstd[:, 0:1],
                                                       in1=ident[:, :], op0=ALU.mult, op1=ALU.add))
                    settle(q, dve.tensor_copy(a_hi[:, :], a_full[:, :]))
                    dve.tensor_tensor(a_lo[:, :], a_full[:, :], a_hi[:, :].bitcast(f32), ALU.subtract).then_inc(a_ready, 1)
                    proj_lo(q, 0)
                    proj_lo(q, 1)

            def macro_step(i, q, conv, attend):
                if isinstance(i, int) and i == 0:
                    steps[0] = 0
                norm = 1 if isinstance(i, int) and i == MACROS - 1 else 0
                for tile in range(4):
                    if conv:
                        last_round = isinstance(i, int) and i == MACROS - 1
                        if not (last_round and tile >= 2):
                            ahead = (tile + 2) % 4
                            split_rows(q - 1, 4 * i + tile + 2, ahead, ahead == 3 and not last_round, ahead == 0)
                        elif tile == 2:
                            dve.wait_ge(conv_done, TILES * q - 3)
                            dve.memset(ring_hi[:, 0:RING:RING - 1, :].bitcast(f32), 0.0)
                            dve.memset(ring_lo[:, 0:RING:RING - 1, :].bitcast(f32), 0.0).then_inc(halo_zeroed, 1)
                    for w in work_of(i, tile, attend):
                        if w[0] == "stats":
                            j = w[1]
                            if j % PER_LOAD == 0:
                                dve.wait_ge(x_loaded[j // PER_LOAD], 16 * (q + 1))
                            ins = dve.bn_stats(stats[:, 6 * j:6 * j + 6], x_chunk(j))
                            if j == TILES - 1:
                                settle(q, ins)
                        elif w[0] in ("gather", "mean", "variance"):
                            group_norm(q, norm, w[0])
                        elif w[0] == "first":
                            start_attention(q)
                        elif w[0] == "attend":
                            j, k = w[1], w[2]
                            if more(j, 1):
                                running_max(q, j + 1, k + 1)
                            dve.wait_ge(xt_hi_ready, TILES * q + j + 1)
                            dve.tensor_tensor(xt[:, :, ONES + CH:GRAM], blocks(xt_ps[:, :]),
                                              xt[:, :, ONES:ONES + CH].bitcast(f32), ALU.subtract).then_inc(xt_lo_ready, 1)
                            dve.wait_ge(et_hi_ready, TILES * q + j + 1)
                            dve.tensor_tensor(et_lo[:, :, :], blocks(et_ps[:, :]), et_hi[:, :, :].bitcast(f32),
                                              ALU.subtract).then_inc(et_lo_ready, 1)
                            if more(j, 2):
                                centre(q, j + 2, k % 2)
                            add_gram(q, j, k)
                        elif w[0] == "chain":
                            chain(q, w[1])
                        elif w[0] == "project":
                            j = w[1]
                            if more(j, 2):
                                proj_lo(q, j + 2)
                            dve.wait_ge(x1_ready, TILES * q + j + 1)
                            ins = dve.bn_stats(stats[:, 6 * j:6 * j + 6], x1_chunk(j))
                            if j == TILES - 1:
                                settle(q, ins)
                                group_norm(q, 1, "gather")

            def transition(q, conv, attend):
                if not attend:
                    return
                split_rows(q, 0, 0, False, False)
                split_rows(q, 1, 1, False, False)
                dve.wait_ge(rstd_ready, 2 * q + 2)
                settle(q, dve.scalar_tensor_tensor(out=wc_mid[:, :], in0=wc_raw[:, CENTRE * CH:(CENTRE + 1) * CH],
                                                   scalar=rstd[:, 1:2], in1=ident[:, :], op0=ALU.mult, op1=ALU.add))
                dve.sem_inc(wc_mid_ready, 1)
                for k, piece in enumerate(W_PIECES):
                    w = slice(piece[0] * CH, (piece[-1] + 1) * CH)
                    dve.wait_ge(wc_hi_ready, len(W_PIECES) * q + k + 1)
                    if piece == [CENTRE]:
                        dve.tensor_tensor(wc_lo[:, w], wc_mid[:, :], wc_hi[:, w].bitcast(f32),
                                          ALU.subtract).then_inc(wc_lo_ready, 1)
                    else:
                        dve.scalar_tensor_tensor(out=wc_lo[:, w], in0=wc_raw[:, w], scalar=rstd[:, 1:2],
                                                 in1=wc_hi[:, w].bitcast(f32), op0=ALU.mult,
                                                 op1=ALU.subtract).then_inc(wc_lo_ready, 1)
                if conv:
                    dve.wait_ge(conv_taken, TILES * q)
                dve.tensor_scalar(out_bias[:, :], shift[:, 1:2], -1.0, None, ALU.mult).then_inc(out_bias_ready, 1)
                assert steps[0] == DVE_STEPS, steps[0]

            dve.wait_ge(weights_loaded, 16 * 9)
            dve.wait_ge(constants_set, 4)
            dve.memset(gram[:, :], 0.0).then_inc(gram_added, 1)
            image_steps(dve, macro_step, transition)

        @block.gpsimd
        def _(pool):
            pool.memset(ring_hi[:, :, :].bitcast(f32), 0.0).then_inc(constants_set, 1)
            pool.memset(ring_lo[:, :, :].bitcast(f32), 0.0).then_inc(constants_set, 1)
            pool.memset(xt[:, :, 0:ONES].bitcast(f32), 1.0).then_inc(constants_set, 1)
            pool.memset(minus_half[:, :], -0.5).then_inc(constants_set, 1)
            pool.wait_ge(constants_set, 4)

            def rstd_of(q, norm):
                pool.wait_ge(var_eps_ready, 2 * q + norm + 1)
                pool.tensor_tensor(rstd[:, norm:norm + 1], var_eps[:, norm:norm + 1], minus_half[:, :],
                                   ALU.pow).then_inc(rstd_ready, 1)

            def key_lo(q, j, slot):
                pool.wait_ge(key_hi_ready, TILES * q + j + 1)
                pool.tensor_tensor(xs_lo[:, slot, :], xc[:, slot, :], xs_hi[:, slot, :].bitcast(f32),
                                   ALU.subtract).then_inc(key_lo_ready, 1)

            def macro_step(i, q, conv, attend):
                for tile in range(4):
                    for w in work_of(i, tile, attend):
                        if w[0] == "attend" and more(w[1], 2):
                            key_lo(q, w[1] + 2, w[2] % 2)
                        elif w[0] == "first":
                            key_lo(q, 0, 0)
                            key_lo(q, 1, 1)
                        elif w[0] == "variance" and i < MACROS - 1:
                            rstd_of(q, 0)

            def transition(q, conv, attend):
                if attend:
                    rstd_of(q, 1)

            image_steps(pool, macro_step, transition)


_ORDER = ["x", "w_key", "w_value", "w_query", "w_out", "b_out", "w_conv", "identity", "group_mean", "head_mask"]


def kernel(x, L0_conv_w_qkv, L0_conv_w_out, L0_conv_b_out, L1_conv_weight):
    import concourse.bacc as bacc
    from concourse.bass_utils import run_bass_kernel_spmd

    x = np.asarray(x)
    w_qkv = np.asarray(L0_conv_w_qkv)
    per_group = CH // GROUPS
    channel = np.arange(CH)
    arrays = {
        "x": x.reshape(IMAGES, CH, PIXELS),
        "w_key": np.ascontiguousarray(w_qkv[CH:2 * CH].T),
        "w_value": np.ascontiguousarray(w_qkv[2 * CH:3 * CH].T),
        "w_query": np.ascontiguousarray(w_qkv[0:CH]),
        "w_out": np.ascontiguousarray(np.asarray(L0_conv_w_out).T),
        "b_out": np.asarray(L0_conv_b_out).reshape(CH, 1),
        "w_conv": np.ascontiguousarray(np.asarray(L1_conv_weight).reshape(TAPS, CH, CH).transpose(2, 0, 1)).reshape(CH, TAPS * CH),
        "identity": np.eye(CH, dtype=np.float32),
        "group_mean": ((channel[:, None] // per_group == channel[None, :] // per_group) / per_group).astype(np.float32),
        "head_mask": (channel[:, None] // (CH // HEADS) == channel[None, :] // (CH // HEADS)).astype(np.float32),
    }
    nc = bacc.Bacc("TRN2", target_bir_lowering=False, num_devices=1)
    args = [nc.dram_tensor(f"in_{n}", arrays[n].shape, mybir.dt.float32, kind="ExternalInput").ap() for n in _ORDER]
    args.append(nc.dram_tensor("out", (IMAGES, CH, PIXELS), mybir.dt.float32, kind="ExternalOutput").ap())
    build(nc, *args)
    result = run_bass_kernel_spmd(nc, [{f"in_{n}": arrays[n] for n in _ORDER}], core_ids=[0])
    return result.results[0]["out"].reshape(x.shape)
```

```python
from contextlib import ExitStack

import numpy as np
import concourse.bass as bass
import concourse.mybir as mybir

IMAGES, CH, HEIGHT, WIDTH = 8, 128, 128, 128
PIXELS = HEIGHT * WIDTH
GROUPS = 32
HEADS = 4
TAPS = 9
KSIZE = 3
EPS = 1e-5

CHUNK = 512
ROWS = CHUNK // WIDTH
TILES = PIXELS // CHUNK
SUB = CHUNK // 128
LOADS = 8
PER_LOAD = TILES // LOADS
STORES = TILES // 2
MACROS = TILES // 4
CT = 2 * CHUNK
CTILES = PIXELS // CT
PAIRS = CT // (2 * WIDTH)
UNITS = 4
M1, M2, M0, M3 = range(UNITS)
PADDED = WIDTH + 2
COLUMNS = (0, 2, 1)
ONES = 1
GRAM = ONES + CH
HUGE = 3.0e38
W_PIECES = [(M1, 0, 1), (M1, 1, 2), (M1, 2, 3), (M2, 0, 2), (M2, 2, 3), (M0, 0, 3), (M3, 0, 3)]
OUT_BIAS_AT = 2
CHAIN = 4


EARLY = 16


def attention_work(macro, tile):
    if macro == 0:
        first = EARLY + 3 * tile
        return [("stats", j) for j in range(first, first + 3)]
    if macro == 1:
        return [[("stats", j) for j in range(EARLY + 12, TILES)] + [("gather",)],
                [("mean",), ("variance",), ("rest",)],
                [("scale",)],
                [("first", 0), ("first", 1), ("first", 2)]][tile]
    if macro == 6:
        return [("rest",)] + [("chain", n) for n in range(CHAIN)] + [("rest",)] if tile == 0 else \
               [("project", j) for j in range(5 * tile - 5, 5 * tile)]
    if macro == 7:
        return [[("project", j) for j in range(15, 21)],
                [("project", j) for j in range(21, 27)],
                [("project", j) for j in range(27, 32)],
                [("mean",), ("variance",), ("rest",)]][tile]


def early_statistics(macro, tile):
    first = PER_LOAD * (4 * macro + tile - 4 * 6 - 3)
    return range(first, first + PER_LOAD) if 0 <= first < EARLY else ()


ATTEND = range(2, 6)


def build(nc, x, w_key, w_value, w_query, w_out, b_out, w_top, w_middle, w_bottom, identity, group_mean, head_mask, out):
    f32, f32r = mybir.dt.float32, mybir.dt.float32r
    ALU, ACT = mybir.AluOpType, mybir.ActivationFunctionType
    ctx = ExitStack()
    with ctx:
        def sb(name, shape, dt=f32):
            return ctx.enter_context(nc.sbuf_tensor(name, shape, dt))

        def ps(name, shape):
            return ctx.enter_context(nc.psum_tensor(name, shape, f32))

        def sem(name):
            return ctx.enter_context(nc.semaphore(name))

        x_img = sb("x_img", [CH, PIXELS])
        x1_img = sb("x1_img", [CH, PIXELS])
        t_rows = sb("t_rows", [CH, UNITS, PAIRS, WIDTH])
        win_hi = sb("win_hi", [CH, UNITS, PAIRS, PADDED], f32r)
        win_lo = sb("win_lo", [CH, UNITS, PAIRS, PADDED], f32r)
        wc_raw = sb("wc_raw", [CH, UNITS, KSIZE * CH])
        wc_g1 = sb("wc_g1", [CH, KSIZE * CH])
        wc_mid = sb("wc_mid", [CH, 2, CH])
        wc_hi = sb("wc_hi", [CH, UNITS, KSIZE * CH], f32r)
        wc_lo = sb("wc_lo", [CH, UNITS, KSIZE * CH], f32r)
        m1_sb = sb("m1_sb", [CH, CHUNK])
        out_stage = sb("out_stage", [CH, 2, CT])
        xc = sb("xc", [CH, 2, CHUNK])
        xs_hi = sb("xs_hi", [CH, 2, CHUNK], f32r)
        xs_lo = sb("xs_lo", [CH, 2, CHUNK], f32r)
        e_chunk = sb("e_chunk", [CH, 2, CHUNK])
        et = sb("et", [128, 2, SUB, CH])
        xt = sb("xt", [128, 2, SUB, GRAM])
        gram = sb("gram", [CH, GRAM])
        neg_max = sb("neg_max", [CH, 4])
        alpha = sb("alpha", [CH, 4])
        wk_raw = sb("wk_raw", [CH, CH])
        wv_sb = sb("wv_sb", [CH, CH])
        wq_sb = sb("wq_sb", [CH, CH])
        wo_sb = sb("wo_sb", [CH, CH])
        ident = sb("ident", [CH, CH])
        half_ident = sb("half_ident", [CH, CH])
        gmat = sb("gmat", [CH, CH])
        mask = sb("mask", [CH, CH])
        wk_tmp = sb("wk_tmp", [CH, CH])
        wk_hi = sb("wk_hi", [CH, CH], f32r)
        wk_lo = sb("wk_lo", [CH, CH], f32r)
        chain_sb = sb("chain_sb", [CH, CH])
        a_full = sb("a_full", [CH, CH])
        x_stats = sb("x_stats", [CH, TILES * 6])
        x1_stats = sb("x1_stats", [CH, TILES * 6])
        moments = sb("moments", [CH, 2, 2])
        shift = sb("shift", [CH, 1])
        x1_shift2 = sb("x1_shift2", [CH, 1])
        x1_mean = sb("x1_mean", [CH, 1])
        dev = sb("dev", [CH, 2])
        var_in = sb("var_in", [CH, 2])
        var_eps = sb("var_eps", [CH, 2])
        rstd = sb("rstd", [CH, 2])
        minus_half = sb("minus_half", [CH, 1])
        b_sb = sb("b_sb", [CH, 1])
        x1_bias = sb("x1_bias", [CH, 1])
        out_bias = sb("out_bias", [CH, 1])
        denom_inv = sb("denom_inv", [CH, 1])

        conv_ps = ps("conv_ps", [CH, 2, CHUNK])
        proj_ps = ps("proj_ps", [CH, 2, CHUNK])
        xt_ps = ps("xt_ps", [128, CHUNK])
        et_ps = ps("et_ps", [128, CHUNK])
        gram_ps = ps("gram_ps", [CH, CHUNK])
        small_ps = ps("small_ps", [CH, CHUNK])
        mean_ps, var_ps, mat_ps = small_ps[:, 0:1], small_ps[:, 4:5], small_ps[:, 128:128 + CH]

        weights_loaded = sem("weights_loaded")
        constants_set = sem("constants_set")
        x_loaded = [sem(f"x_loaded{g}") for g in range(LOADS)]
        stage_free = [sem(f"stage_free{s}") for s in range(2)]
        moments_ready = sem("moments_ready")
        mean_done = sem("mean_done")
        shift_ready = sem("shift_ready")
        var_in_ready = sem("var_in_ready")
        var_done = sem("var_done")
        var_eps_ready = sem("var_eps_ready")
        rstd_ready = sem("rstd_ready")
        start_set = sem("start_set")
        wk_ready = sem("wk_ready")
        xc_ready = sem("xc_ready")
        key_hi_ready = sem("key_hi_ready")
        key_lo_ready = sem("key_lo_ready")
        key_done = sem("key_done")
        max_ready = sem("max_ready")
        exp_ready = sem("exp_ready")
        alpha_ready = sem("alpha_ready")
        xt_done = sem("xt_done")
        et_done = sem("et_done")
        xt_ready = sem("xt_ready")
        et_ready = sem("et_ready")
        gram_done = sem("gram_done")
        gram_added = sem("gram_added")
        chain_in = sem("chain_in")
        chain_out = sem("chain_out")
        a_ready = sem("a_ready")
        proj_in_ready = sem("proj_in_ready")
        proj_done = sem("proj_done")
        x1_ready = sem("x1_ready")
        rows_made = sem("rows_made")
        win_hi_ready = sem("win_hi_ready")
        win_lo_ready = sem("win_lo_ready")
        wc_mid_ready = sem("wc_mid_ready")
        wc_hi_ready = sem("wc_hi_ready")
        wc_lo_ready = sem("wc_lo_ready")
        unit_done = sem("unit_done")
        m1_taken = sem("m1_taken")
        m2_taken = sem("m2_taken")
        y_made = sem("y_made")
        out_bias_ready = sem("out_bias_ready")
        weights_combined = sem("weights_combined")
        dve_settled = sem("dve_settled")
        DVE_STEPS = 7

        def x_chunk(j):
            return x_img[:, bass.ds(j * CHUNK, CHUNK)]

        def x1_chunk(j):
            return x1_img[:, bass.ds(j * CHUNK, CHUNK)]

        def rows(ap):
            return ap.rearrange("c (r w) -> c r w", w=WIDTH)

        def row_pairs(start, pairs=PAIRS):
            return x1_img[:, bass.ds(start, 2 * pairs * WIDTH)].rearrange("c (p two w) -> c two p w", two=2, w=WIDTH)

        def stage_rows(slot, which):
            return out_stage[:, slot, :].rearrange("c (p two w) -> c two p w", two=2, w=WIDTH)[:, which]

        def next_units(i, tile, last_round):
            t = 2 * i + tile // 2
            if tile % 2 == 0:
                return [(t, M0), (t, M3)]
            if last_round and tile == 3:
                return []
            return [(t + 1, M1), (t + 1, M2)]

        def places(work):
            if not work or work[0][0] == "stats":
                return (0, 0), 0
            return {2: ((0, 0), 1), 3: ((0, 0), 2), 5: ((1, 2), 3), 6: ((1, 2), 3)}.get(len(work), ((0, 0), 0))

        def known(t, value):
            return isinstance(t, int) and t == value

        def blocks(ap):
            return ap.rearrange("n (s c) -> n s c", c=CH)

        def image_steps(engine, macro_step, transition):
            def step(q, conv, attend):
                def macro(i):
                    macro_step(i, q, conv, attend)
                if attend:
                    for i in range(ATTEND.start):
                        macro(i)
                    with engine.Fori(ATTEND.start, ATTEND.stop - 1) as i:
                        macro(i)
                    for i in range(ATTEND.stop - 1, MACROS):
                        macro(i)
                else:
                    macro(0)
                    with engine.Fori(1, MACROS - 1) as i:
                        macro(i)
                    macro(MACROS - 1)
                transition(q, conv, attend)
            step(0, False, True)
            with engine.Fori(1, IMAGES - 1) as q:
                step(q, True, True)
            step(IMAGES - 1, True, True)
            step(IMAGES, True, False)

        def work_of(i, tile, attend):
            if not attend:
                return []
            if not isinstance(i, int) or i in ATTEND:
                j = (i - ATTEND.start) * 8 + 2 * tile
                return [("attend", j, 2 * tile), ("attend", j + 1, 2 * tile + 1)]
            return attention_work(i, tile)

        def more(j, ahead):
            return not isinstance(j, int) or j + ahead < TILES

        block = ctx.enter_context(nc.Block())

        @block.sync
        def _(sp):
            def load(q, g):
                sp.dma_start(x_img[:, g * PER_LOAD * CHUNK:(g + 1) * PER_LOAD * CHUNK],
                             x[q, :, g * PER_LOAD * CHUNK:(g + 1) * PER_LOAD * CHUNK]).then_inc(x_loaded[g], 16)

            def reload(q, g):
                sp.wait_ge(proj_in_ready, TILES * (q - 1) + PER_LOAD * (g + 1))
                load(q, g)

            def store(p, u, slot):
                sp.wait_ge(y_made, 2 * CTILES * p + 2 * u + 2)
                sp.dma_start(out[p, :, bass.ds(u * CT, CT)], out_stage[:, slot, :]).then_inc(stage_free[slot], 16)

            def early_stores(p, count):
                with sp.Fori(0, count // 2) as v:
                    store(p, 2 * v, 0)
                    store(p, 2 * v + 1, 1)

            for g in range(LOADS):
                load(0, g)
            for g in range(LOADS):
                reload(1, g)

            def late(p, reloading):
                q = p + 2
                for what, n in [("r", 0), ("s", 12), ("r", 1), ("r", 2), ("r", 3), ("s", 13), ("r", 4), ("r", 5),
                                ("r", 6), ("s", 14), ("r", 7), ("s", 15)]:
                    if what == "s":
                        store(p, n, n % 2)
                    elif reloading:
                        reload(q, n)
            with sp.Fori(0, IMAGES - 2) as p:
                early_stores(p, 12)
                late(p, True)
            for p in (IMAGES - 2, IMAGES - 1):
                early_stores(p, 12)
                late(p, False)
            for s in range(2):
                sp.wait_ge(stage_free[s], 16 * (IMAGES * STORES // 2 + 1))

        @block.tensor
        def _(pe):
            def three(ps_out, w_hi, w_lo, m_hi, m_lo, start, stop):
                pe.matmul(ps_out, w_hi, m_hi, start=start, stop=False)
                pe.matmul(ps_out, w_hi, m_lo, start=False, stop=False)
                return pe.matmul(ps_out, w_lo, m_hi, start=False, stop=stop)

            def conv_part(p, i, tile, part, parts):
                t = 2 * i + tile // 2
                first = M1 if tile % 2 == 0 else M0
                entries = [(unit, c) for unit in (first, first + 1) for c in range(KSIZE)]
                for unit, c in entries[len(entries) * part // parts:len(entries) * (part + 1) // parts]:
                    if c == 0:
                        pe.wait_ge(win_lo_ready, UNITS * (CTILES * p + t) + unit + 1)
                        if unit == M0:
                            pe.wait_ge(m1_taken, CTILES * p + t + 1)
                        elif unit == M3:
                            pe.wait_ge(m2_taken, CTILES * p + t + 1)
                        elif not known(t, 0):
                            pe.wait_ge(y_made, 2 * (CTILES * p + t - 1) + unit - M1 + 1)
                        elif unit == M2:
                            pe.wait_ge(out_bias_ready, p + 1)
                    if known(t, 0):
                        for n, (piece_unit, c0, _) in enumerate(W_PIECES):
                            if (piece_unit, c0) == (unit, c):
                                pe.wait_ge(wc_lo_ready, len(W_PIECES) * p + n + 1)
                    w = slice(c * CH, (c + 1) * CH)
                    dx = COLUMNS[c]
                    last = three(rows(conv_ps[:, unit % 2, :]), wc_hi[:, unit, w], wc_lo[:, unit, w],
                                 win_hi[:, unit, :, dx:dx + WIDTH], win_lo[:, unit, :, dx:dx + WIDTH],
                                 c == 0, c == KSIZE - 1)
                    if c == KSIZE - 1:
                        last.then_inc(unit_done, 1)

            def key(q, j, slot):
                pe.wait_ge(key_lo_ready, TILES * q + j + 1)
                three(proj_ps[:, slot, :], wk_hi[:, :], wk_lo[:, :], xs_hi[:, slot, :], xs_lo[:, slot, :],
                      True, True).then_inc(key_done, 1)

            def turn_x(q, j, slot):
                pe.wait_ge(xc_ready, TILES * q + j + 1)
                if not (isinstance(j, int) and j == 0):
                    pe.wait_ge(xt_ready, TILES * q + j)
                for s in range(SUB):
                    last = pe.transpose(xt_ps[:, s * 128:(s + 1) * 128], xc[:, slot, s * 128:(s + 1) * 128], ident[:, :])
                last.then_inc(xt_done, 1)

            def turn_e(q, j, slot):
                pe.wait_ge(exp_ready, TILES * q + j + 1)
                if not (isinstance(j, int) and j == 0):
                    pe.wait_ge(et_ready, TILES * q + j)
                for s in range(SUB):
                    last = pe.transpose(et_ps[:, s * 128:(s + 1) * 128], e_chunk[:, slot, s * 128:(s + 1) * 128], ident[:, :])
                last.then_inc(et_done, 1)

            def gram_product(q, j, slot):
                pe.wait_ge(xt_ready, TILES * q + j + 1)
                pe.wait_ge(et_ready, TILES * q + j + 1)
                pe.wait_ge(gram_added, (TILES + 1) * q + j + 1)
                for s in range(SUB):
                    last = pe.matmul(gram_ps[:, 0:GRAM], et[:, slot, s, :], xt[:, slot, s, :],
                                     start=(s == 0), stop=(s == SUB - 1))
                last.then_inc(gram_done, 1)

            def chain(q, n):
                pe.wait_ge(chain_in, CHAIN * q + n + 1)
                if n == 0:
                    last = pe.transpose(mat_ps, gram[:, ONES:ONES + CH], ident[:, :])
                elif n == 1:
                    last = pe.matmul(mat_ps, wv_sb[:, :], chain_sb[:, :], start=True, stop=True)
                elif n == 2:
                    last = pe.matmul(mat_ps, chain_sb[:, :], wo_sb[:, :], start=True, stop=True)
                else:
                    last = pe.matmul(mat_ps, wq_sb[:, :], chain_sb[:, :], start=True, stop=True)
                last.then_inc(chain_out, 1)

            def project(q, j):
                if j == 0:
                    pe.wait_ge(a_ready, q + 1)
                pe.wait_ge(proj_in_ready, TILES * q + j + 1)
                if j >= 2:
                    pe.wait_ge(x1_ready, TILES * q + j - 1)
                pe.matmul(proj_ps[:, j % 2, :], a_full[:, :], xc[:, j % 2, :], start=True, stop=True).then_inc(proj_done, 1)

            def macro_step(i, q, conv, attend):
                for tile in range(4):
                    work = [w for w in work_of(i, tile, attend) if w[0] not in ("stats", "gather")]
                    norm = 0 if isinstance(i, int) and i < MACROS - 1 else 1
                    parts = max(1, len(work))
                    for part in range(parts):
                        w = work[part] if work else ("rest",)
                        if w[0] == "attend":
                            j, slot = w[1], w[2] % 2
                            if more(j, 1):
                                turn_x(q, j + 1, 1 - slot)
                            if more(j, 2):
                                key(q, j + 2, slot)
                            if more(j, 1):
                                turn_e(q, j + 1, 1 - slot)
                        elif w[0] == "chain":
                            chain(q, w[1])
                        elif w[0] == "project":
                            project(q, w[1])
                        elif w == ("first", 0):
                            pe.wait_ge(wk_ready, q + 1)
                            key(q, 0, 0)
                            turn_x(q, 0, 0)
                        elif w == ("first", 1):
                            key(q, 1, 1)
                        elif w == ("first", 2):
                            turn_e(q, 0, 0)
                        if conv:
                            conv_part(q - 1, i, tile, part, parts)
                        if w[0] == "attend":
                            gram_product(q, w[1], w[2] % 2)
                        elif w[0] == "mean":
                            pe.wait_ge(moments_ready, 2 * q + norm + 1)
                            pe.matmul(mean_ps, gmat[:, :], moments[:, norm, 0:1], start=True, stop=True).then_inc(mean_done, 1)
                        elif w[0] == "variance":
                            pe.wait_ge(var_in_ready, 2 * q + norm + 1)
                            pe.matmul(var_ps, gmat[:, :], var_in[:, norm:norm + 1], start=True, stop=True).then_inc(var_done, 1)

            pe.wait_ge(weights_loaded, 16 * 11)
            pe.wait_ge(constants_set, 4)
            image_steps(pe, macro_step, lambda q, conv, attend: None)

        @block.scalar
        def _(act):
            for dst, src in ((ident, identity), (gmat, group_mean), (mask, head_mask), (wk_raw, w_key), (wv_sb, w_value),
                             (wq_sb, w_query), (wo_sb, w_out), (b_sb, b_out), (wc_raw[:, M0, :], w_top), (wc_g1, w_middle),
                             (wc_raw[:, M3, :], w_bottom)):
                act.dma_start(dst[:, :], src).then_inc(weights_loaded, 16)

            for slot in range(2):
                act.sem_inc(stage_free[slot], 16)

            def exp_chunk(q, j, k):
                act.wait_ge(max_ready, TILES * q + j + 1)
                act.activation(e_chunk[:, k % 2, :], proj_ps[:, k % 2, :], ACT.Exp, bias=neg_max[:, k % 4:k % 4 + 1],
                               scale=-1.0).then_inc(exp_ready, 1)
                act.activation(alpha[:, k % 4:k % 4 + 1], neg_max[:, (k - 1) % 4:(k - 1) % 4 + 1], ACT.Exp,
                               bias=neg_max[:, k % 4:k % 4 + 1], scale=-1.0).then_inc(alpha_ready, 1)

            def key_hi(q, j, slot):
                act.wait_ge(xc_ready, TILES * q + j + 1)
                if not (isinstance(j, int) and j < 2):
                    act.wait_ge(key_done, TILES * q + j - 1)
                act.activation(xs_hi[:, slot, :], xc[:, slot, :], ACT.Identity).then_inc(key_hi_ready, 1)

            def take_xt(q, j, slot):
                act.wait_ge(xt_done, TILES * q + j + 1)
                act.activation(xt[:, slot, :, ONES:GRAM], blocks(xt_ps[:, :]), ACT.Identity).then_inc(xt_ready, 1)

            def take_et(q, j, slot):
                act.wait_ge(et_done, TILES * q + j + 1)
                act.activation(et[:, slot, :, :], blocks(et_ps[:, :]), ACT.Identity).then_inc(et_ready, 1)

            def proj_in(q, j):
                if j >= 2:
                    act.wait_ge(proj_done, TILES * q + j - 1)
                else:
                    act.wait_ge(key_done, TILES * q + TILES - 1 + j)
                    act.wait_ge(xt_done, TILES * q + TILES - 1 + j)
                act.activation(xc[:, j % 2, :], x_chunk(j), ACT.Identity, bias=shift[:, 0:1]).then_inc(proj_in_ready, 1)

            def take_x1(q, conv, j):
                act.wait_ge(proj_done, TILES * q + j + 1)
                if conv:
                    act.wait_ge(rows_made, UNITS * (CTILES * (q - 1) + min((j + 1) // 2, CTILES - 1) + 1))
                act.activation(x1_chunk(j), proj_ps[:, j % 2, :], ACT.Identity, bias=x1_bias[:, 0:1]).then_inc(x1_ready, 1)

            def window_hi(p, t, unit, fresh=False):
                u = UNITS * (CTILES * p + t) + unit
                act.wait_ge(rows_made, u + 1)
                if not fresh:
                    act.wait_ge(unit_done, u - UNITS + 1)
                act.activation(win_hi[:, unit, :, 1:1 + WIDTH], t_rows[:, unit, :, :], ACT.Identity,
                               bias=x1_shift2[:, 0:1] if unit == M1 else 0.0).then_inc(win_hi_ready, 1)

            def take_m1(p, t):
                act.wait_ge(unit_done, UNITS * (CTILES * p + t) + M1 + 1)
                if not known(t, 0):
                    act.wait_ge(m2_taken, CTILES * p + t)
                act.activation(m1_sb[:, :], conv_ps[:, M1 % 2, :], ACT.Identity).then_inc(m1_taken, 1)

            def macro_step(i, q, conv, attend):
                last_round = isinstance(i, int) and i == MACROS - 1

                for tile in range(4):
                    work = work_of(i, tile, attend)
                    windows_at, middle_at = places(work)
                    prepared = next_units(i, tile, last_round) if conv else []
                    for n, w in enumerate(work or [("rest",)]):
                        for (t, unit), at in zip(prepared, windows_at):
                            if n == at:
                                window_hi(q - 1, t, unit, fresh=known(t, 0))
                        if conv and n == middle_at and tile % 2 == 0:
                            take_m1(q - 1, 2 * i + tile // 2)
                        if w[0] == "attend":
                            j, k = w[1], w[2]
                            if more(j, 1):
                                take_xt(q, j + 1, (k + 1) % 2)
                            if more(j, 3):
                                key_hi(q, j + 3, (k + 3) % 2)
                            if more(j, 1):
                                take_et(q, j + 1, (k + 1) % 2)
                            if more(j, 2):
                                exp_chunk(q, j + 2, k + 2)
                        elif w[0] == "scale":
                            key_hi(q, 0, 0)
                            key_hi(q, 1, 1)
                        elif w == ("first", 0):
                            exp_chunk(q, 0, 0)
                            take_xt(q, 0, 0)
                        elif w == ("first", 1):
                            key_hi(q, 2, 0)
                            exp_chunk(q, 1, 1)
                        elif w == ("first", 2):
                            take_et(q, 0, 0)
                        elif w == ("chain", 0):
                            proj_in(q, 0)
                            proj_in(q, 1)
                        elif w[0] == "project":
                            take_x1(q, conv, w[1])
                            if more(w[1], 2):
                                proj_in(q, w[1] + 2)

            def transition(q, conv, attend):
                if attend:
                    window_hi(q, 0, M1, fresh=not conv)
                    window_hi(q, 0, M2, fresh=not conv)
                    act.wait_ge(rstd_ready, 2 * q + 2)
                    for n, (unit, c0, c1) in enumerate(W_PIECES):
                        w = slice(c0 * CH, c1 * CH)
                        if conv:
                            act.wait_ge(unit_done, UNITS * (CTILES * q - 1) + unit + 1)
                        if unit in (M1, M2) and c0 == KSIZE - 1:
                            act.wait_ge(wc_mid_ready, q + 1)
                            act.activation(wc_hi[:, unit, w], wc_mid[:, unit, :], ACT.Identity).then_inc(wc_hi_ready, 1)
                        else:
                            act.activation(wc_hi[:, unit, w], wc_raw[:, unit, w], ACT.Identity,
                                           scale=rstd[:, 1:2]).then_inc(wc_hi_ready, 1)

            act.wait_ge(constants_set, 4)
            act.wait_ge(weights_loaded, 16 * 11)
            image_steps(act, macro_step, transition)

        @block.vector
        def _(dve):
            steps = [0]

            def settle(q, instruction):
                steps[0] += 1
                instruction.then_inc(dve_settled, 1)
                dve.wait_ge(dve_settled, DVE_STEPS * q + steps[0])

            def group_norm(q, norm, stage):
                n = 2 * q + norm + 1
                if stage == "gather":
                    if norm == 0:
                        dve.memset(neg_max[:, 3:4], HUGE).then_inc(start_set, 1)
                    else:
                        dve.memset(gram[:, :], 0.0).then_inc(gram_added, 1)
                    dve.bn_aggr(moments[:, norm, :], (x1_stats if norm else x_stats)[:, :]).then_inc(moments_ready, 1)
                elif stage == "mean":
                    dve.wait_ge(mean_done, n)
                    dve.wait_ge(moments_ready, n)
                    if norm == 0:
                        dve.tensor_scalar(shift[:, :], mean_ps, -1.0, None, ALU.mult).then_inc(shift_ready, 1)
                    else:
                        dve.tensor_scalar(x1_shift2[:, :], mean_ps, -2.0, None, ALU.mult)
                        dve.tensor_copy(x1_mean[:, :], mean_ps).then_inc(shift_ready, 1)
                    settle(q, dve.tensor_tensor(dev[:, norm:norm + 1], moments[:, norm, 0:1], mean_ps, ALU.subtract))
                    dve.scalar_tensor_tensor(out=var_in[:, norm:norm + 1], in0=dev[:, norm:norm + 1],
                                             scalar=dev[:, norm:norm + 1], in1=moments[:, norm, 1:2],
                                             op0=ALU.mult, op1=ALU.add).then_inc(var_in_ready, 1)
                else:
                    dve.wait_ge(var_done, n)
                    dve.tensor_scalar(var_eps[:, norm:norm + 1], var_ps, EPS, None, ALU.add).then_inc(var_eps_ready, 1)

            def x_statistics(q, j):
                if j % PER_LOAD == 0:
                    dve.wait_ge(x_loaded[j // PER_LOAD], 16 * (q + 1))
                return dve.bn_stats(x_stats[:, 6 * j:6 * j + 6], x_chunk(j))

            def centre(q, j, slot):
                if not (isinstance(j, int) and j < 2):
                    dve.wait_ge(xt_done, TILES * q + j - 1)
                dve.tensor_scalar(xc[:, slot, :], x_chunk(j), shift[:, 0:1], None, ALU.add).then_inc(xc_ready, 1)

            def running_max(q, j, k):
                dve.wait_ge(key_done, TILES * q + j + 1)
                if not (isinstance(j, int) and j == 0):
                    dve.wait_ge(max_ready, TILES * q + j)
                dve.tensor_scalar(e_chunk[:, k % 2, :], proj_ps[:, k % 2, :], 1.0, neg_max[:, (k - 1) % 4:(k - 1) % 4 + 1],
                                  ALU.mult, ALU.min, accum_out=neg_max[:, k % 4:k % 4 + 1]).then_inc(max_ready, 1)

            def key_lo(q, j, slot):
                dve.wait_ge(key_hi_ready, TILES * q + j + 1)
                dve.tensor_tensor(xs_lo[:, slot, :], xc[:, slot, :], xs_hi[:, slot, :].bitcast(f32),
                                  ALU.subtract).then_inc(key_lo_ready, 1)

            def add_gram(q, j, k):
                dve.wait_ge(gram_done, TILES * q + j + 1)
                dve.wait_ge(alpha_ready, TILES * q + j + 1)
                dve.wait_ge(gram_added, (TILES + 1) * q + j + 1)
                dve.scalar_tensor_tensor(out=gram[:, :], in0=gram[:, :], scalar=alpha[:, k % 4:k % 4 + 1],
                                         in1=gram_ps[:, 0:GRAM], op0=ALU.mult, op1=ALU.add).then_inc(gram_added, 1)

            def window_lo(p, t, unit):
                dve.wait_ge(win_hi_ready, UNITS * (CTILES * p + t) + unit + 1)
                hi = win_hi[:, unit, :, 1:1 + WIDTH].bitcast(f32)
                lo = win_lo[:, unit, :, 1:1 + WIDTH]
                if unit == M1:
                    dve.scalar_tensor_tensor(out=lo, in0=t_rows[:, unit, :, :], scalar=x1_shift2[:, 0:1], in1=hi,
                                             op0=ALU.add, op1=ALU.subtract).then_inc(win_lo_ready, 1)
                else:
                    dve.tensor_tensor(lo, t_rows[:, unit, :, :], hi, ALU.subtract).then_inc(win_lo_ready, 1)

            def take_m2(p, t, slot, i):
                dve.wait_ge(unit_done, UNITS * (CTILES * p + t) + M2 + 1)
                dve.wait_ge(m1_taken, CTILES * p + t + 1)
                dve.wait_ge(stage_free[slot], 16 * (MACROS * p + i + 1))
                dve.tensor_tensor(stage_rows(slot, 0), rows(m1_sb[:, :]), rows(conv_ps[:, M2 % 2, :]), ALU.add)
                dve.tensor_tensor(stage_rows(slot, 1), rows(m1_sb[:, :]), rows(conv_ps[:, M2 % 2, :]),
                                  ALU.subtract).then_inc(m2_taken, 1)

            def finish_rows(p, t, slot, which):
                unit = M3 if which else M0
                dve.wait_ge(unit_done, UNITS * (CTILES * p + t) + unit + 1)
                dve.wait_ge(m2_taken, CTILES * p + t + 1)
                dve.scalar_tensor_tensor(out=stage_rows(slot, which), in0=rows(conv_ps[:, unit % 2, :]),
                                         scalar=out_bias[:, 0:1], in1=stage_rows(slot, which), op0=ALU.add,
                                         op1=ALU.add).then_inc(y_made, 1)

            def prepare_weights():
                dve.wait_ge(weights_loaded, 16 * 11)
                ends = wc_raw[:, M1, :]
                dve.tensor_tensor(ends, wc_raw[:, M0, :], wc_raw[:, M3, :], ALU.add).then_inc(weights_combined, 1)
                dve.wait_ge(weights_combined, 1)
                dve.tensor_tensor(wc_raw[:, M2, :], ends, wc_g1[:, :], ALU.subtract).then_inc(weights_combined, 1)
                dve.tensor_tensor(ends, ends, wc_g1[:, :], ALU.add).then_inc(weights_combined, 1)
                dve.wait_ge(weights_combined, 3)
                dve.tensor_scalar(wc_raw[:, M1:M2 + 1, :], wc_raw[:, M1:M2 + 1, :], 0.5, None,
                                  ALU.mult).then_inc(weights_combined, 1)
                dve.tensor_scalar(half_ident[:, :], ident[:, :], 0.5, None, ALU.mult).then_inc(weights_combined, 1)
                dve.wait_ge(weights_combined, 5)

            def start_attention(q):
                dve.wait_ge(weights_loaded, 16 * 11)
                centre(q, 0, 0)
                centre(q, 1, 1)
                dve.tensor_tensor(x1_bias[:, :], b_sb[:, :], shift[:, 0:1], ALU.subtract)
                dve.wait_ge(rstd_ready, 2 * q + 1)
                settle(q, dve.tensor_scalar(wk_tmp[:, :], wk_raw[:, :], rstd[:, 0:1], -1.0, ALU.mult, ALU.mult))
                settle(q, dve.tensor_copy(wk_hi[:, :], wk_tmp[:, :]))
                dve.tensor_tensor(wk_lo[:, :], wk_tmp[:, :], wk_hi[:, :].bitcast(f32), ALU.subtract).then_inc(wk_ready, 1)
                key_lo(q, 0, 0)
                key_lo(q, 1, 1)

            def chain(q, n):
                if n == 0:
                    dve.wait_ge(gram_added, (TILES + 1) * (q + 1))
                    settle(q, dve.reciprocal(denom_inv[:, :], gram[:, 0:1]))
                    dve.tensor_scalar(gram[:, ONES:ONES + CH], gram[:, ONES:ONES + CH], denom_inv[:, 0:1], None,
                                      ALU.mult).then_inc(chain_in, 1)
                    dve.wait_ge(chain_out, CHAIN * q + 1)
                    dve.tensor_scalar(chain_sb[:, :], mat_ps, rstd[:, 0:1], None, ALU.mult).then_inc(chain_in, 1)
                elif n == 1:
                    dve.wait_ge(chain_out, CHAIN * q + 2)
                    dve.tensor_tensor(chain_sb[:, :], mat_ps, mask[:, :], ALU.mult).then_inc(chain_in, 1)
                elif n == 2:
                    dve.wait_ge(chain_out, CHAIN * q + 3)
                    dve.tensor_copy(chain_sb[:, :], mat_ps).then_inc(chain_in, 1)
                else:
                    dve.wait_ge(chain_out, CHAIN * q + 4)
                    dve.scalar_tensor_tensor(out=a_full[:, :], in0=mat_ps, scalar=rstd[:, 0:1], in1=ident[:, :],
                                             op0=ALU.mult, op1=ALU.add).then_inc(a_ready, 1)

            def macro_step(i, q, conv, attend):
                if known(i, 0):
                    steps[0] = 0
                last_round = known(i, MACROS - 1)
                norm = 1 if last_round else 0

                for tile in range(4):
                    work = work_of(i, tile, attend)
                    windows_at, middle_at = places(work)
                    prepared = next_units(i, tile, last_round) if conv else []
                    t, slot = 2 * i + tile // 2, tile // 2
                    if known(q, 0) and known(i, 0) and tile == 0:
                        for j in range(EARLY):
                            x_statistics(q, j)
                    for n, w in enumerate(work or [("rest",)]):
                        if conv and n == windows_at[0]:
                            if tile % 2 == 1:
                                take_m2(q - 1, t, slot, i)
                            elif not known(t, 0):
                                finish_rows(q - 1, t - 1, 1 - slot, 1)
                        for (ahead, unit), at in zip(prepared, windows_at):
                            if n == at:
                                window_lo(q - 1, ahead, unit)
                        if conv and n == middle_at and tile % 2 == 1:
                            finish_rows(q - 1, t, slot, 0)
                        if w[0] == "stats":
                            j = w[1]
                            ins = x_statistics(q, j)
                            if j == TILES - 1:
                                settle(q, ins)
                        elif w[0] in ("gather", "mean", "variance"):
                            group_norm(q, norm, w[0])
                        elif w[0] == "scale":
                            start_attention(q)
                        elif w == ("first", 0):
                            dve.wait_ge(start_set, q + 1)
                            running_max(q, 0, 0)
                            centre(q, 2, 0)
                            key_lo(q, 2, 0)
                        elif w == ("first", 1):
                            running_max(q, 1, 1)
                        elif w[0] == "attend":
                            j, k = w[1], w[2]
                            if more(j, 3):
                                centre(q, j + 3, (k + 3) % 2)
                            if more(j, 2):
                                running_max(q, j + 2, k + 2)
                            if more(j, 3):
                                key_lo(q, j + 3, (k + 3) % 2)
                            add_gram(q, j, k)
                        elif w[0] == "chain":
                            if w[1] == 0 and not conv:
                                prepare_weights()
                            chain(q, w[1])
                        elif w[0] == "project":
                            j = w[1]
                            dve.wait_ge(x1_ready, TILES * q + j + 1)
                            ins = dve.bn_stats(x1_stats[:, 6 * j:6 * j + 6], x1_chunk(j))
                            if j == TILES - 1:
                                settle(q, ins)
                                group_norm(q, 1, "gather")
                    if attend and isinstance(i, int) and not known(q, IMAGES - 1):
                        for j in early_statistics(i, tile):
                            x_statistics(q + 1, j)

            def transition(q, conv, attend):
                if attend:
                    window_lo(q, 0, M1)
                    window_lo(q, 0, M2)
                    dve.wait_ge(rstd_ready, 2 * q + 2)
                    centre_column = slice((KSIZE - 1) * CH, KSIZE * CH)
                    dve.scalar_tensor_tensor(out=wc_mid[:, M1, :], in0=wc_raw[:, M1, centre_column],
                                             scalar=rstd[:, 1:2], in1=half_ident[:, :], op0=ALU.mult, op1=ALU.add)
                    dve.scalar_tensor_tensor(out=wc_mid[:, M2, :], in0=wc_raw[:, M2, centre_column],
                                             scalar=rstd[:, 1:2], in1=half_ident[:, :], op0=ALU.mult,
                                             op1=ALU.subtract).then_inc(wc_mid_ready, 1)
                    for n, (unit, c0, c1) in enumerate(W_PIECES):
                        w = slice(c0 * CH, c1 * CH)
                        dve.wait_ge(wc_hi_ready, len(W_PIECES) * q + n + 1)
                        if unit in (M1, M2) and c0 == KSIZE - 1:
                            dve.wait_ge(wc_mid_ready, q + 1)
                            dve.tensor_tensor(wc_lo[:, unit, w], wc_mid[:, unit, :], wc_hi[:, unit, w].bitcast(f32),
                                              ALU.subtract).then_inc(wc_lo_ready, 1)
                        else:
                            dve.scalar_tensor_tensor(out=wc_lo[:, unit, w], in0=wc_raw[:, unit, w], scalar=rstd[:, 1:2],
                                                     in1=wc_hi[:, unit, w].bitcast(f32), op0=ALU.mult,
                                                     op1=ALU.subtract).then_inc(wc_lo_ready, 1)
                        if n == OUT_BIAS_AT:
                            if conv:
                                finish_rows(q - 1, CTILES - 1, 1, 1)
                                dve.wait_ge(y_made, 2 * CTILES * q)
                            dve.tensor_copy(out_bias[:, :], x1_mean[:, :]).then_inc(out_bias_ready, 1)
                    assert steps[0] == DVE_STEPS, steps[0]
                elif conv:
                    finish_rows(q - 1, CTILES - 1, 1, 1)

            dve.wait_ge(constants_set, 4)
            dve.memset(gram[:, :], 0.0).then_inc(gram_added, 1)
            image_steps(dve, macro_step, transition)

        @block.gpsimd
        def _(pool):
            pool.memset(win_hi[:, :, :, :].bitcast(f32), 0.0).then_inc(constants_set, 1)
            pool.memset(win_lo[:, :, :, :].bitcast(f32), 0.0).then_inc(constants_set, 1)
            pool.memset(xt[:, :, :, 0:ONES], 1.0).then_inc(constants_set, 1)
            pool.memset(minus_half[:, :], -0.5).then_inc(constants_set, 1)
            pool.wait_ge(constants_set, 4)

            def rstd_of(q, norm):
                pool.wait_ge(var_eps_ready, 2 * q + norm + 1)
                pool.tensor_tensor(rstd[:, norm:norm + 1], var_eps[:, norm:norm + 1], minus_half[:, :],
                                   ALU.pow).then_inc(rstd_ready, 1)

            def make_rows(p, t, unit, fresh=False):
                if not fresh and unit in (M1, M0):
                    pool.wait_ge(win_lo_ready, UNITS * (CTILES * p + t - 1) + unit + 2)
                dst = t_rows[:, unit, :, :]
                here = row_pairs(t * CT)
                if unit == M1:
                    pool.tensor_tensor(dst, here[:, 0], here[:, 1], ALU.add).then_inc(rows_made, 1)
                elif unit == M2:
                    pool.tensor_tensor(dst, here[:, 1], here[:, 0], ALU.subtract).then_inc(rows_made, 1)
                elif unit == M0 and known(t, 0):
                    pool.tensor_scalar(dst[:, 0, :], here[:, 1, 0], -1.0, x1_mean[:, 0:1], ALU.mult, ALU.add)
                    pool.tensor_tensor(dst[:, 1:, :], row_pairs(WIDTH, PAIRS - 1)[:, 0], here[:, 1, 1:],
                                       ALU.subtract).then_inc(rows_made, 1)
                elif unit == M0:
                    pool.tensor_tensor(dst, row_pairs(t * CT - WIDTH)[:, 0], here[:, 1], ALU.subtract).then_inc(rows_made, 1)
                elif known(t, CTILES - 1):
                    pool.tensor_scalar(dst[:, PAIRS - 1, :], here[:, 0, PAIRS - 1], -1.0, x1_mean[:, 0:1], ALU.mult, ALU.add)
                    pool.tensor_tensor(dst[:, 0:PAIRS - 1, :], here[:, 0, 1:], here[:, 0, 0:PAIRS - 1],
                                       ALU.subtract).then_inc(rows_made, 1)
                else:
                    pool.tensor_tensor(dst, row_pairs(t * CT + 2 * WIDTH)[:, 0], here[:, 0],
                                       ALU.subtract).then_inc(rows_made, 1)

            def macro_step(i, q, conv, attend):
                for tile in range(4):
                    if conv:
                        for t, unit in next_units(i, tile, known(i, MACROS - 1)):
                            make_rows(q - 1, t, unit, fresh=known(t, 0))
                    for w in work_of(i, tile, attend):
                        if w[0] == "variance" and i < MACROS - 1:
                            rstd_of(q, 0)

            def transition(q, conv, attend):
                if attend:
                    pool.wait_ge(shift_ready, 2 * q + 2)
                    if conv:
                        pool.wait_ge(win_lo_ready, UNITS * CTILES * q)
                    make_rows(q, 0, M1, fresh=True)
                    make_rows(q, 0, M2, fresh=True)
                    rstd_of(q, 1)

            image_steps(pool, macro_step, transition)


_ORDER = ["x", "w_key", "w_value", "w_query", "w_out", "b_out", "w_top", "w_middle", "w_bottom", "identity", "group_mean", "head_mask"]


def kernel(x, L0_conv_w_qkv, L0_conv_w_out, L0_conv_b_out, L1_conv_weight):
    import concourse.bacc as bacc
    from concourse.bass_utils import run_bass_kernel_spmd

    x = np.asarray(x)
    w_qkv = np.asarray(L0_conv_w_qkv)
    per_group = CH // GROUPS
    channel = np.arange(CH)
    w_rows = np.asarray(L1_conv_weight).reshape(KSIZE, KSIZE, CH, CH)[:, list(COLUMNS)].transpose(0, 3, 1, 2)
    w_rows = np.ascontiguousarray(w_rows).reshape(KSIZE, CH, KSIZE * CH)
    arrays = {
        "x": x.reshape(IMAGES, CH, PIXELS),
        "w_key": np.ascontiguousarray(w_qkv[CH:2 * CH].T),
        "w_value": np.ascontiguousarray(w_qkv[2 * CH:3 * CH].T),
        "w_query": np.ascontiguousarray(w_qkv[0:CH]),
        "w_out": np.ascontiguousarray(np.asarray(L0_conv_w_out).T),
        "b_out": np.asarray(L0_conv_b_out).reshape(CH, 1),
        "w_top": w_rows[0], "w_middle": w_rows[1], "w_bottom": w_rows[2],
        "identity": np.eye(CH, dtype=np.float32),
        "group_mean": ((channel[:, None] // per_group == channel[None, :] // per_group) / per_group).astype(np.float32),
        "head_mask": (channel[:, None] // (CH // HEADS) == channel[None, :] // (CH // HEADS)).astype(np.float32),
    }
    nc = bacc.Bacc("TRN2", target_bir_lowering=False, num_devices=1, dynamic_dma_scratch_size=2048)
    args = [nc.dram_tensor(f"in_{n}", arrays[n].shape, mybir.dt.float32, kind="ExternalInput").ap() for n in _ORDER]
    args.append(nc.dram_tensor("out", (IMAGES, CH, PIXELS), mybir.dt.float32, kind="ExternalOutput").ap())
    build(nc, *args)
    result = run_bass_kernel_spmd(nc, [{f"in_{n}": arrays[n] for n in _ORDER}], core_ids=[0])
    return result.results[0]["out"].reshape(x.shape)
```

```python
from contextlib import ExitStack

import numpy as np
import concourse.bass as bass
import concourse.mybir as mybir

IMAGES, CH, HEIGHT, WIDTH = 8, 128, 128, 128
PIXELS = HEIGHT * WIDTH
GROUPS = 32
HEADS = 4
KSIZE = 3
EPS = 1e-5

CHUNK = 512
TILES = PIXELS // CHUNK
SUB = CHUNK // 128
LOADS = 8
PER_LOAD = TILES // LOADS
CT = 2 * CHUNK
CTILES = PIXELS // CT
MACROS = CTILES // 2
PAIRS = CT // (2 * WIDTH)
UNITS = 4
M1, M2, M0, M3 = range(UNITS)
PADDED = WIDTH + 2
COLUMNS = (0, 2, 1)
ONES = 1
GRAM = ONES + CH
HUGE = 3.0e38
W_PIECES = [(M1, 0, 1), (M1, 1, 2), (M1, 2, 3), (M2, 0, 2), (M2, 2, 3), (M0, 0, 3), (M3, 0, 3)]
NEXT_UNIT_AT = 3
CHAIN = 4


ATTEND = range(2, 5)
PER_SLOT = 3
FIRST_PROJECTION = 20
PROJECTED = (3, 3, 3, 3, 3, 3, 3, 3, 3, 3, 2)
EARLY = (0, 3, 3, 2, 3, 3, 3, 3, 3, 3)
STATISTICS = (0, 2, 2, 2, 0)
assert sum(PROJECTED) == sum(EARLY) + sum(STATISTICS) == TILES


def attention_work(macro, tile):
    if macro == 0:
        first = sum(EARLY) + sum(STATISTICS[:tile])
        return [("stats", j) for j in range(first, first + STATISTICS[tile])]
    if macro == 1:
        return [[("stats", j) for j in range(TILES - STATISTICS[4], TILES)] + [("gather",)],
                [("mean",), ("variance",), ("centre",)],
                [("scale",), ("rest",)],
                [("first", 0), ("first", 1), ("rest",), ("rest",), ("first", 2), ("rest",)]][tile]
    slot = 4 * macro + tile - FIRST_PROJECTION
    if slot < -1:
        first = PER_SLOT * (4 * (macro - ATTEND.start) + tile)
        return [("attend", j, j) for j in range(first, min(first + PER_SLOT, TILES))]
    if slot == -1:
        return [("rest",)] + [("chain", n) for n in range(CHAIN)] + [("rest",)]
    if slot < len(PROJECTED):
        first = sum(PROJECTED[:slot])
        return [("project", j) for j in range(first, first + PROJECTED[slot])]
    return [("mean",), ("variance",), ("rest",)]


def early_statistics(macro, tile):
    slot = 4 * macro + tile - FIRST_PROJECTION
    return range(sum(EARLY[:slot]), sum(EARLY[:slot + 1])) if 0 <= slot < len(EARLY) else ()


def build(nc, x, w_key, w_value, w_query, w_out, b_out, w_top, w_middle, w_bottom, identity, group_mean, head_mask, out):
    f32, f32r = mybir.dt.float32, mybir.dt.float32r
    ALU, ACT = mybir.AluOpType, mybir.ActivationFunctionType
    ctx = ExitStack()
    with ctx:
        def sb(name, shape, dt=f32):
            return ctx.enter_context(nc.sbuf_tensor(name, shape, dt))

        def ps(name, shape):
            return ctx.enter_context(nc.psum_tensor(name, shape, f32))

        def sem(name):
            return ctx.enter_context(nc.semaphore(name))

        x_img = sb("x_img", [CH, PIXELS])
        x1_img = sb("x1_img", [CH, PIXELS])
        t_rows = sb("t_rows", [CH, UNITS, PAIRS, WIDTH])
        win_hi = sb("win_hi", [CH, UNITS, PAIRS, PADDED], f32r)
        win_lo = sb("win_lo", [CH, UNITS, PAIRS, PADDED], f32r)
        wc_raw = sb("wc_raw", [CH, UNITS, KSIZE * CH])
        wc_g1 = sb("wc_g1", [CH, KSIZE * CH])
        wc_mid = sb("wc_mid", [CH, 2, CH])
        wc_hi = sb("wc_hi", [CH, UNITS, KSIZE * CH], f32r)
        wc_lo = sb("wc_lo", [CH, UNITS, KSIZE * CH], f32r)
        m1_sb = sb("m1_sb", [CH, CHUNK])
        out_stage = sb("out_stage", [CH, 2, CT])
        xc = sb("xc", [CH, 2, CHUNK])
        xs_hi = sb("xs_hi", [CH, 2, CHUNK], f32r)
        xs_lo = sb("xs_lo", [CH, 2, CHUNK], f32r)
        e_chunk = sb("e_chunk", [CH, 2, CHUNK])
        et = sb("et", [128, 2, SUB, CH])
        xt = sb("xt", [128, 2, SUB, GRAM])
        gram = sb("gram", [CH, GRAM])
        neg_max = sb("neg_max", [CH, 4])
        alpha = sb("alpha", [CH, 4])
        wk_raw = sb("wk_raw", [CH, CH])
        wv_sb = sb("wv_sb", [CH, CH])
        wq_sb = sb("wq_sb", [CH, CH])
        wo_sb = sb("wo_sb", [CH, CH])
        ident = sb("ident", [CH, CH])
        half_ident = sb("half_ident", [CH, CH])
        gmat = sb("gmat", [CH, CH])
        mask = sb("mask", [CH, CH])
        wk_tmp = sb("wk_tmp", [CH, CH])
        wk_hi = sb("wk_hi", [CH, CH], f32r)
        wk_lo = sb("wk_lo", [CH, CH], f32r)
        chain_sb = sb("chain_sb", [CH, CH])
        a_full = sb("a_full", [CH, CH])
        x_stats = sb("x_stats", [CH, TILES * 6])
        x1_stats = sb("x1_stats", [CH, TILES * 6])
        moments = sb("moments", [CH, 2, 2])
        shift = sb("shift", [CH, 1])
        x1_shift2 = sb("x1_shift2", [CH, 1])
        x1_mean = sb("x1_mean", [CH, 1])
        dev = sb("dev", [CH, 2])
        var_in = sb("var_in", [CH, 2])
        var_eps = sb("var_eps", [CH, 2])
        rstd = sb("rstd", [CH, 2])
        minus_half = sb("minus_half", [CH, 1])
        b_sb = sb("b_sb", [CH, 1])
        x1_bias = sb("x1_bias", [CH, 1])
        out_bias = sb("out_bias", [CH, 1])
        denom_inv = sb("denom_inv", [CH, 1])

        conv_ps = ps("conv_ps", [CH, 2, CHUNK])
        proj_ps = ps("proj_ps", [CH, 2, CHUNK])
        xt_ps = ps("xt_ps", [128, CHUNK])
        et_ps = ps("et_ps", [128, CHUNK])
        gram_ps = ps("gram_ps", [CH, CHUNK])
        small_ps = ps("small_ps", [CH, CHUNK])
        mean_ps, var_ps, mat_ps = small_ps[:, 0:1], small_ps[:, 4:5], small_ps[:, 128:128 + CH]

        weights_loaded = sem("weights_loaded")
        constants_set = sem("constants_set")
        x_loaded = [sem(f"x_loaded{g}") for g in range(LOADS)]
        stage_free = [sem(f"stage_free{s}") for s in range(2)]
        moments_ready = sem("moments_ready")
        mean_done = sem("mean_done")
        shift_ready = sem("shift_ready")
        var_in_ready = sem("var_in_ready")
        var_done = sem("var_done")
        var_eps_ready = sem("var_eps_ready")
        rstd_ready = sem("rstd_ready")
        start_set = sem("start_set")
        wk_ready = sem("wk_ready")
        xc_ready = sem("xc_ready")
        key_hi_ready = sem("key_hi_ready")
        key_lo_ready = sem("key_lo_ready")
        key_done = sem("key_done")
        max_ready = sem("max_ready")
        exp_ready = sem("exp_ready")
        alpha_ready = sem("alpha_ready")
        xt_done = sem("xt_done")
        et_done = sem("et_done")
        xt_ready = sem("xt_ready")
        et_ready = sem("et_ready")
        gram_done = sem("gram_done")
        gram_added = sem("gram_added")
        chain_in = sem("chain_in")
        chain_out = sem("chain_out")
        a_ready = sem("a_ready")
        proj_in_ready = sem("proj_in_ready")
        proj_done = sem("proj_done")
        x1_ready = sem("x1_ready")
        rows_made = sem("rows_made")
        win_hi_ready = sem("win_hi_ready")
        win_lo_ready = sem("win_lo_ready")
        wc_mid_ready = sem("wc_mid_ready")
        wc_hi_ready = sem("wc_hi_ready")
        wc_lo_ready = sem("wc_lo_ready")
        unit_done = sem("unit_done")
        m1_taken = sem("m1_taken")
        m2_taken = sem("m2_taken")
        y_made = sem("y_made")
        out_bias_ready = sem("out_bias_ready")
        weights_combined = sem("weights_combined")
        dve_settled = sem("dve_settled")
        DVE_STEPS = 7

        def x_chunk(j):
            return x_img[:, bass.ds(j * CHUNK, CHUNK)]

        def x1_chunk(j):
            return x1_img[:, bass.ds(j * CHUNK, CHUNK)]

        def rows(ap):
            return ap.rearrange("c (r w) -> c r w", w=WIDTH)

        def row_pairs(start, pairs=PAIRS):
            return x1_img[:, bass.ds(start, 2 * pairs * WIDTH)].rearrange("c (p two w) -> c two p w", two=2, w=WIDTH)

        def stage_rows(slot, which):
            return out_stage[:, slot, :].rearrange("c (p two w) -> c two p w", two=2, w=WIDTH)[:, which]

        def next_units(i, tile, last_round):
            t = 2 * i + tile // 2
            if tile % 2 == 0:
                return [(t, M0), (t, M3)]
            if last_round and tile == 3:
                return []
            return [(t + 1, M1), (t + 1, M2)]

        def places(work):
            if ("chain", 0) in work:
                return None, (4, 5), 4
            if not work or work[0][0] == "stats":
                return 0, (0, 0), 0
            if ("first", 0) in work:
                return 0, (2, 3), 3
            if ("scale",) in work:
                return 0, (1, 1), 1
            if ("mean",) in work:
                return 0, (1, 2), 2
            return {2: (0, (0, 1), 1), 3: (0, (0, 1), 2), 6: (1, (1, 2), 4)}.get(len(work), (0, (0, 0), 0))

        def known(t, value):
            return isinstance(t, int) and t == value

        def blocks(ap):
            return ap.rearrange("n (s c) -> n s c", c=CH)

        def image_steps(engine, macro_step, transition):
            def step(q, conv, attend):
                def macro(i):
                    macro_step(i, q, conv, attend)
                if attend:
                    for i in range(ATTEND.start):
                        macro(i)
                    with engine.Fori(ATTEND.start, ATTEND.stop - 1) as i:
                        macro(i)
                    for i in range(ATTEND.stop - 1, MACROS):
                        macro(i)
                else:
                    macro(0)
                    with engine.Fori(1, MACROS - 1) as i:
                        macro(i)
                    macro(MACROS - 1)
                transition(q, conv, attend)
            step(0, False, True)
            with engine.Fori(1, IMAGES - 1) as q:
                step(q, True, True)
            step(IMAGES - 1, True, True)
            step(IMAGES, True, False)

        def work_of(i, tile, attend):
            if not attend:
                return []
            if not isinstance(i, int):
                first = (i - ATTEND.start) * (4 * PER_SLOT)
                return [("attend", first + k, k) for k in range(PER_SLOT * tile, PER_SLOT * (tile + 1))]
            return attention_work(i, tile)

        def more(j, ahead):
            return not isinstance(j, int) or j + ahead < TILES

        block = ctx.enter_context(nc.Block())

        @block.sync
        def _(sp):
            def load(q, g):
                sp.dma_start(x_img[:, g * PER_LOAD * CHUNK:(g + 1) * PER_LOAD * CHUNK],
                             x[q, :, g * PER_LOAD * CHUNK:(g + 1) * PER_LOAD * CHUNK]).then_inc(x_loaded[g], 16)

            def reload(q, g):
                sp.wait_ge(proj_in_ready, TILES * (q - 1) + PER_LOAD * (g + 1))
                load(q, g)

            def store(p, u, slot):
                sp.wait_ge(y_made, 2 * CTILES * p + 2 * u + 2)
                sp.dma_start(out[p, :, bass.ds(u * CT, CT)], out_stage[:, slot, :]).then_inc(stage_free[slot], 16)

            def early_stores(p, count):
                with sp.Fori(0, count // 2) as v:
                    store(p, 2 * v, 0)
                    store(p, 2 * v + 1, 1)

            for g in range(LOADS):
                load(0, g)
            for g in range(LOADS):
                reload(1, g)

            def late(p, reloading):
                q = p + 2
                for what, n in [("s", 8), ("s", 9), ("r", 0), ("r", 1), ("s", 10), ("r", 2), ("s", 11), ("r", 3),
                                ("r", 4), ("s", 12), ("r", 5), ("s", 13), ("r", 6), ("r", 7), ("s", 14), ("s", 15)]:
                    if what == "s":
                        store(p, n, n % 2)
                    elif reloading:
                        reload(q, n)
            with sp.Fori(0, IMAGES - 2) as p:
                early_stores(p, 8)
                late(p, True)
            for p in (IMAGES - 2, IMAGES - 1):
                early_stores(p, 8)
                late(p, False)
            for s in range(2):
                sp.wait_ge(stage_free[s], 16 * (IMAGES * CTILES // 2 + 1))

        @block.tensor
        def _(pe):
            def three(ps_out, w_hi, w_lo, m_hi, m_lo, start, stop):
                pe.matmul(ps_out, w_hi, m_hi, start=start, stop=False)
                pe.matmul(ps_out, w_hi, m_lo, start=False, stop=False)
                return pe.matmul(ps_out, w_lo, m_hi, start=False, stop=stop)

            def conv_part(p, i, tile, part, parts):
                t = 2 * i + tile // 2
                first = M1 if tile % 2 == 0 else M0
                entries = [(unit, c) for unit in (first, first + 1) for c in range(KSIZE)]
                for unit, c in entries[len(entries) * part // parts:len(entries) * (part + 1) // parts]:
                    if c == 0:
                        pe.wait_ge(win_lo_ready, UNITS * (CTILES * p + t) + unit + 1)
                        if unit == M0:
                            pe.wait_ge(m1_taken, CTILES * p + t + 1)
                        elif unit == M3:
                            pe.wait_ge(m2_taken, CTILES * p + t + 1)
                        elif not known(t, 0):
                            pe.wait_ge(y_made, 2 * (CTILES * p + t - 1) + unit - M1 + 1)
                    if known(t, 0):
                        for n, (piece_unit, c0, _) in enumerate(W_PIECES):
                            if (piece_unit, c0) == (unit, c):
                                pe.wait_ge(wc_lo_ready, len(W_PIECES) * p + n + 1)
                    w = slice(c * CH, (c + 1) * CH)
                    dx = COLUMNS[c]
                    last = three(rows(conv_ps[:, unit % 2, :]), wc_hi[:, unit, w], wc_lo[:, unit, w],
                                 win_hi[:, unit, :, dx:dx + WIDTH], win_lo[:, unit, :, dx:dx + WIDTH],
                                 c == 0, c == KSIZE - 1)
                    if c == KSIZE - 1:
                        last.then_inc(unit_done, 1)

            def key(q, j, slot):
                pe.wait_ge(key_lo_ready, TILES * q + j + 1)
                three(proj_ps[:, slot, :], wk_hi[:, :], wk_lo[:, :], xs_hi[:, slot, :], xs_lo[:, slot, :],
                      True, True).then_inc(key_done, 1)

            def turn_x(q, j, slot):
                pe.wait_ge(xc_ready, TILES * q + j + 1)
                if not (isinstance(j, int) and j == 0):
                    pe.wait_ge(xt_ready, TILES * q + j)
                for s in range(SUB):
                    last = pe.transpose(xt_ps[:, s * 128:(s + 1) * 128], xc[:, slot, s * 128:(s + 1) * 128], ident[:, :])
                last.then_inc(xt_done, 1)

            def turn_e(q, j, slot):
                pe.wait_ge(exp_ready, TILES * q + j + 1)
                if not (isinstance(j, int) and j == 0):
                    pe.wait_ge(et_ready, TILES * q + j)
                for s in range(SUB):
                    last = pe.transpose(et_ps[:, s * 128:(s + 1) * 128], e_chunk[:, slot, s * 128:(s + 1) * 128], ident[:, :])
                last.then_inc(et_done, 1)

            def gram_product(q, j, slot):
                pe.wait_ge(xt_ready, TILES * q + j + 1)
                pe.wait_ge(et_ready, TILES * q + j + 1)
                pe.wait_ge(gram_added, (TILES + 1) * q + j + 1)
                for s in range(SUB):
                    last = pe.matmul(gram_ps[:, 0:GRAM], et[:, slot, s, :], xt[:, slot, s, :],
                                     start=(s == 0), stop=(s == SUB - 1))
                last.then_inc(gram_done, 1)

            def chain(q, n):
                pe.wait_ge(chain_in, CHAIN * q + n + 1)
                if n == 0:
                    last = pe.transpose(mat_ps, gram[:, ONES:ONES + CH], ident[:, :])
                elif n == 1:
                    last = pe.matmul(mat_ps, wv_sb[:, :], chain_sb[:, :], start=True, stop=True)
                elif n == 2:
                    last = pe.matmul(mat_ps, chain_sb[:, :], wo_sb[:, :], start=True, stop=True)
                else:
                    last = pe.matmul(mat_ps, wq_sb[:, :], chain_sb[:, :], start=True, stop=True)
                last.then_inc(chain_out, 1)

            def project(q, j):
                if j == 0:
                    pe.wait_ge(a_ready, q + 1)
                pe.wait_ge(proj_in_ready, TILES * q + j + 1)
                if j >= 2:
                    pe.wait_ge(x1_ready, TILES * q + j - 1)
                pe.matmul(proj_ps[:, j % 2, :], a_full[:, :], xc[:, j % 2, :], start=True, stop=True).then_inc(proj_done, 1)

            def macro_step(i, q, conv, attend):
                for tile in range(4):
                    work = [w for w in work_of(i, tile, attend) if w[0] not in ("stats", "gather")]
                    norm = 0 if isinstance(i, int) and i < MACROS - 1 else 1
                    parts = max(1, len(work))
                    for part in range(parts):
                        w = work[part] if work else ("rest",)
                        if w[0] == "attend":
                            j, slot = w[1], w[2] % 2
                            if more(j, 1):
                                turn_x(q, j + 1, 1 - slot)
                            if more(j, 2):
                                key(q, j + 2, slot)
                            if more(j, 1):
                                turn_e(q, j + 1, 1 - slot)
                        elif w[0] == "project" and w[1] > 0:
                            project(q, w[1])
                        elif w == ("first", 0):
                            pe.wait_ge(wk_ready, q + 1)
                            key(q, 0, 0)
                            turn_x(q, 0, 0)
                        elif w == ("first", 1):
                            key(q, 1, 1)
                        elif w == ("first", 2):
                            turn_e(q, 0, 0)
                        if conv:
                            conv_part(q - 1, i, tile, part, parts)
                        if w[0] == "chain":
                            chain(q, w[1])
                        elif w == ("project", 0):
                            project(q, 0)
                        if w[0] == "attend":
                            gram_product(q, w[1], w[2] % 2)
                        elif w[0] == "mean":
                            pe.wait_ge(moments_ready, 2 * q + norm + 1)
                            pe.matmul(mean_ps, gmat[:, :], moments[:, norm, 0:1], start=True, stop=True).then_inc(mean_done, 1)
                        elif w[0] == "variance":
                            pe.wait_ge(var_in_ready, 2 * q + norm + 1)
                            pe.matmul(var_ps, gmat[:, :], var_in[:, norm:norm + 1], start=True, stop=True).then_inc(var_done, 1)

            pe.wait_ge(weights_loaded, 16 * 11)
            pe.wait_ge(constants_set, 4)
            image_steps(pe, macro_step, lambda q, conv, attend: None)

        @block.scalar
        def _(act):
            for dst, src in ((ident, identity), (gmat, group_mean), (mask, head_mask), (wk_raw, w_key), (wv_sb, w_value),
                             (wq_sb, w_query), (wo_sb, w_out), (b_sb, b_out), (wc_raw[:, M0, :], w_top), (wc_g1, w_middle),
                             (wc_raw[:, M3, :], w_bottom)):
                act.dma_start(dst[:, :], src).then_inc(weights_loaded, 16)

            for slot in range(2):
                act.sem_inc(stage_free[slot], 16)

            def exp_chunk(q, j, k):
                act.wait_ge(max_ready, TILES * q + j + 1)
                act.activation(e_chunk[:, k % 2, :], proj_ps[:, k % 2, :], ACT.Exp, bias=neg_max[:, k % 4:k % 4 + 1],
                               scale=-1.0).then_inc(exp_ready, 1)
                act.activation(alpha[:, k % 4:k % 4 + 1], neg_max[:, (k - 1) % 4:(k - 1) % 4 + 1], ACT.Exp,
                               bias=neg_max[:, k % 4:k % 4 + 1], scale=-1.0).then_inc(alpha_ready, 1)

            def key_hi(q, j, slot):
                act.wait_ge(xc_ready, TILES * q + j + 1)
                if not (isinstance(j, int) and j < 2):
                    act.wait_ge(key_done, TILES * q + j - 1)
                act.activation(xs_hi[:, slot, :], xc[:, slot, :], ACT.Identity).then_inc(key_hi_ready, 1)

            def take_xt(q, j, slot):
                act.wait_ge(xt_done, TILES * q + j + 1)
                act.activation(xt[:, slot, :, ONES:GRAM], blocks(xt_ps[:, :]), ACT.Identity).then_inc(xt_ready, 1)

            def take_et(q, j, slot):
                act.wait_ge(et_done, TILES * q + j + 1)
                act.activation(et[:, slot, :, :], blocks(et_ps[:, :]), ACT.Identity).then_inc(et_ready, 1)

            def proj_in(q, j):
                if j >= 2:
                    act.wait_ge(proj_done, TILES * q + j - 1)
                else:
                    act.wait_ge(key_done, TILES * q + TILES - 1 + j)
                    act.wait_ge(xt_done, TILES * q + TILES - 1 + j)
                act.activation(xc[:, j % 2, :], x_chunk(j), ACT.Identity, bias=shift[:, 0:1]).then_inc(proj_in_ready, 1)

            def take_x1(q, conv, j):
                act.wait_ge(proj_done, TILES * q + j + 1)
                if conv:
                    act.wait_ge(rows_made, UNITS * (CTILES * (q - 1) + min((j + 1) // 2, CTILES - 1) + 1))
                act.activation(x1_chunk(j), proj_ps[:, j % 2, :], ACT.Identity, bias=x1_bias[:, 0:1]).then_inc(x1_ready, 1)

            def window_hi(p, t, unit, fresh=False):
                u = UNITS * (CTILES * p + t) + unit
                act.wait_ge(rows_made, u + 1)
                if not fresh:
                    act.wait_ge(unit_done, u - UNITS + 1)
                act.activation(win_hi[:, unit, :, 1:1 + WIDTH], t_rows[:, unit, :, :], ACT.Identity,
                               bias=x1_shift2[:, 0:1] if unit == M2 else 0.0).then_inc(win_hi_ready, 1)

            def take_m1(p, t):
                act.wait_ge(unit_done, UNITS * (CTILES * p + t) + M1 + 1)
                if not known(t, 0):
                    act.wait_ge(m2_taken, CTILES * p + t)
                act.activation(m1_sb[:, :], conv_ps[:, M1 % 2, :], ACT.Identity).then_inc(m1_taken, 1)

            def macro_step(i, q, conv, attend):
                last_round = isinstance(i, int) and i == MACROS - 1

                for tile in range(4):
                    work = work_of(i, tile, attend)
                    sums_at, windows_at, middle_at = places(work)
                    prepared = next_units(i, tile, last_round) if conv else []
                    for n, w in enumerate(work or [("rest",)]):
                        for (t, unit), at in zip(prepared, windows_at):
                            if n == at and not (known(t, 0) and unit == M0):
                                window_hi(q - 1, t, unit, fresh=known(t, 0))
                        if conv and n == middle_at and tile % 2 == 0:
                            take_m1(q - 1, 2 * i + tile // 2)
                        if w[0] == "attend":
                            j, k = w[1], w[2]
                            if more(j, 1):
                                take_xt(q, j + 1, (k + 1) % 2)
                            if more(j, 3):
                                key_hi(q, j + 3, (k + 3) % 2)
                            if more(j, 1):
                                take_et(q, j + 1, (k + 1) % 2)
                            if more(j, 2):
                                exp_chunk(q, j + 2, k + 2)
                        elif w[0] == "centre":
                            act.wait_ge(shift_ready, 2 * q + 1)
                            act.activation(xc[:, 0, :], x_chunk(0), ACT.Identity, bias=shift[:, 0:1]).then_inc(xc_ready, 1)
                            act.activation(xc[:, 1, :], x_chunk(1), ACT.Identity, bias=shift[:, 0:1]).then_inc(xc_ready, 1)
                        elif w[0] == "scale":
                            key_hi(q, 0, 0)
                            key_hi(q, 1, 1)
                        elif w == ("first", 0):
                            exp_chunk(q, 0, 0)
                            take_xt(q, 0, 0)
                        elif w == ("first", 1):
                            exp_chunk(q, 1, 1)
                            key_hi(q, 2, 0)
                        elif w == ("first", 2):
                            take_et(q, 0, 0)
                        elif w == ("chain", 0):
                            proj_in(q, 0)
                            proj_in(q, 1)
                        elif w[0] == "project":
                            take_x1(q, conv, w[1])
                            if more(w[1], 2):
                                proj_in(q, w[1] + 2)

            def transition(q, conv, attend):
                if attend:
                    window_hi(q, 0, M1, fresh=not conv)
                    act.wait_ge(shift_ready, 2 * q + 2)
                    window_hi(q, 0, M2, fresh=not conv)
                    act.wait_ge(rstd_ready, 2 * q + 2)
                    for n, (unit, c0, c1) in enumerate(W_PIECES):
                        w = slice(c0 * CH, c1 * CH)
                        if n == len(W_PIECES) - 1:
                            window_hi(q, 0, M0, fresh=not conv)
                        if conv:
                            act.wait_ge(unit_done, UNITS * (CTILES * q - 1) + unit + 1)
                        if unit in (M1, M2) and c0 == KSIZE - 1:
                            act.wait_ge(wc_mid_ready, 2 * q + unit - M1 + 1)
                            act.activation(wc_hi[:, unit, w], wc_mid[:, unit, :], ACT.Identity).then_inc(wc_hi_ready, 1)
                        else:
                            act.activation(wc_hi[:, unit, w], wc_raw[:, unit, w], ACT.Identity,
                                           scale=rstd[:, 1:2]).then_inc(wc_hi_ready, 1)

            act.wait_ge(constants_set, 4)
            act.wait_ge(weights_loaded, 16 * 11)
            image_steps(act, macro_step, transition)

        @block.vector
        def _(dve):
            steps = [0]

            def settle(q, instruction):
                steps[0] += 1
                instruction.then_inc(dve_settled, 1)
                dve.wait_ge(dve_settled, DVE_STEPS * q + steps[0])

            def group_norm(q, norm, stage):
                n = 2 * q + norm + 1
                if stage == "gather":
                    if norm == 0:
                        dve.memset(neg_max[:, 3:4], HUGE).then_inc(start_set, 1)
                    else:
                        dve.memset(gram[:, :], 0.0).then_inc(gram_added, 1)
                    dve.bn_aggr(moments[:, norm, :], (x1_stats if norm else x_stats)[:, :]).then_inc(moments_ready, 1)
                elif stage == "mean":
                    dve.wait_ge(mean_done, n)
                    dve.wait_ge(moments_ready, n)
                    if norm == 0:
                        dve.tensor_scalar(shift[:, :], mean_ps, -1.0, None, ALU.mult).then_inc(shift_ready, 1)
                    else:
                        dve.tensor_scalar(x1_shift2[:, :], mean_ps, -2.0, None, ALU.mult)
                        dve.tensor_copy(x1_mean[:, :], mean_ps).then_inc(shift_ready, 1)
                    settle(q, dve.tensor_tensor(dev[:, norm:norm + 1], moments[:, norm, 0:1], mean_ps, ALU.subtract))
                    dve.scalar_tensor_tensor(out=var_in[:, norm:norm + 1], in0=dev[:, norm:norm + 1],
                                             scalar=dev[:, norm:norm + 1], in1=moments[:, norm, 1:2],
                                             op0=ALU.mult, op1=ALU.add).then_inc(var_in_ready, 1)
                else:
                    dve.wait_ge(var_done, n)
                    dve.tensor_scalar(var_eps[:, norm:norm + 1], var_ps, EPS, None, ALU.add).then_inc(var_eps_ready, 1)

            def x_statistics(q, j):
                if j % PER_LOAD == 0:
                    dve.wait_ge(x_loaded[j // PER_LOAD], 16 * (q + 1))
                return dve.bn_stats(x_stats[:, 6 * j:6 * j + 6], x_chunk(j))

            def centre(q, j, slot):
                if not (isinstance(j, int) and j < 2):
                    dve.wait_ge(xt_done, TILES * q + j - 1)
                dve.tensor_scalar(xc[:, slot, :], x_chunk(j), shift[:, 0:1], None, ALU.add).then_inc(xc_ready, 1)

            def running_max(q, j, k):
                dve.wait_ge(key_done, TILES * q + j + 1)
                if not (isinstance(j, int) and j == 0):
                    dve.wait_ge(max_ready, TILES * q + j)
                dve.tensor_scalar(e_chunk[:, k % 2, :], proj_ps[:, k % 2, :], 1.0, neg_max[:, (k - 1) % 4:(k - 1) % 4 + 1],
                                  ALU.mult, ALU.min, accum_out=neg_max[:, k % 4:k % 4 + 1]).then_inc(max_ready, 1)

            def key_lo(q, j, slot):
                dve.wait_ge(key_hi_ready, TILES * q + j + 1)
                dve.tensor_tensor(xs_lo[:, slot, :], xc[:, slot, :], xs_hi[:, slot, :].bitcast(f32),
                                  ALU.subtract).then_inc(key_lo_ready, 1)

            def add_gram(q, j, k):
                dve.wait_ge(gram_done, TILES * q + j + 1)
                dve.wait_ge(alpha_ready, TILES * q + j + 1)
                dve.wait_ge(gram_added, (TILES + 1) * q + j + 1)
                dve.scalar_tensor_tensor(out=gram[:, :], in0=gram[:, :], scalar=alpha[:, k % 4:k % 4 + 1],
                                         in1=gram_ps[:, 0:GRAM], op0=ALU.mult, op1=ALU.add).then_inc(gram_added, 1)

            def window_lo(p, t, unit):
                dve.wait_ge(win_hi_ready, UNITS * (CTILES * p + t) + unit + 1)
                hi = win_hi[:, unit, :, 1:1 + WIDTH].bitcast(f32)
                lo = win_lo[:, unit, :, 1:1 + WIDTH]
                if unit == M2:
                    dve.scalar_tensor_tensor(out=lo, in0=t_rows[:, unit, :, :], scalar=x1_shift2[:, 0:1], in1=hi,
                                             op0=ALU.add, op1=ALU.subtract).then_inc(win_lo_ready, 1)
                else:
                    dve.tensor_tensor(lo, t_rows[:, unit, :, :], hi, ALU.subtract).then_inc(win_lo_ready, 1)

            def take_m2(p, t, slot, i):
                dve.wait_ge(unit_done, UNITS * (CTILES * p + t) + M2 + 1)
                dve.wait_ge(m1_taken, CTILES * p + t + 1)
                dve.wait_ge(stage_free[slot], 16 * (MACROS * p + i + 1))
                dve.tensor_tensor(stage_rows(slot, 0), rows(m1_sb[:, :]), rows(conv_ps[:, M2 % 2, :]), ALU.add)
                dve.tensor_tensor(stage_rows(slot, 1), rows(conv_ps[:, M2 % 2, :]), rows(m1_sb[:, :]),
                                  ALU.subtract).then_inc(m2_taken, 1)

            def finish_rows(p, t, slot, which):
                unit = M3 if which else M0
                dve.wait_ge(unit_done, UNITS * (CTILES * p + t) + unit + 1)
                dve.wait_ge(m2_taken, CTILES * p + t + 1)
                dve.wait_ge(out_bias_ready, p + 1)
                dve.scalar_tensor_tensor(out=stage_rows(slot, which), in0=rows(conv_ps[:, unit % 2, :]),
                                         scalar=out_bias[:, 0:1], in1=stage_rows(slot, which), op0=ALU.add,
                                         op1=ALU.add).then_inc(y_made, 1)

            def prepare_weights():
                dve.wait_ge(weights_loaded, 16 * 11)
                ends = wc_raw[:, M1, :]
                dve.tensor_tensor(ends, wc_raw[:, M0, :], wc_raw[:, M3, :], ALU.add).then_inc(weights_combined, 1)
                dve.wait_ge(weights_combined, 1)
                dve.tensor_tensor(wc_raw[:, M2, :], ends, wc_g1[:, :], ALU.add).then_inc(weights_combined, 1)
                dve.tensor_tensor(ends, ends, wc_g1[:, :], ALU.subtract).then_inc(weights_combined, 1)
                dve.wait_ge(weights_combined, 3)
                dve.tensor_scalar(wc_raw[:, M1:M2 + 1, :], wc_raw[:, M1:M2 + 1, :], 0.5, None,
                                  ALU.mult).then_inc(weights_combined, 1)
                dve.tensor_scalar(half_ident[:, :], ident[:, :], 0.5, None, ALU.mult).then_inc(weights_combined, 1)
                dve.wait_ge(weights_combined, 5)

            def start_attention(q):
                dve.wait_ge(weights_loaded, 16 * 11)
                dve.tensor_tensor(x1_bias[:, :], b_sb[:, :], shift[:, 0:1], ALU.subtract)
                dve.wait_ge(rstd_ready, 2 * q + 1)
                settle(q, dve.tensor_scalar(wk_tmp[:, :], wk_raw[:, :], rstd[:, 0:1], -1.0, ALU.mult, ALU.mult))
                settle(q, dve.tensor_copy(wk_hi[:, :], wk_tmp[:, :]))
                dve.tensor_tensor(wk_lo[:, :], wk_tmp[:, :], wk_hi[:, :].bitcast(f32), ALU.subtract).then_inc(wk_ready, 1)
                key_lo(q, 0, 0)
                key_lo(q, 1, 1)

            def chain(q, n, beside):
                if n == 0:
                    dve.wait_ge(gram_added, (TILES + 1) * (q + 1))
                    settle(q, dve.reciprocal(denom_inv[:, :], gram[:, 0:1]))
                    dve.tensor_scalar(gram[:, ONES:ONES + CH], gram[:, ONES:ONES + CH], denom_inv[:, 0:1], None,
                                      ALU.mult).then_inc(chain_in, 1)
                    beside()
                    dve.wait_ge(chain_out, CHAIN * q + 1)
                    dve.tensor_scalar(chain_sb[:, :], mat_ps, rstd[:, 0:1], None, ALU.mult).then_inc(chain_in, 1)
                elif n == 1:
                    dve.wait_ge(chain_out, CHAIN * q + 2)
                    dve.tensor_tensor(chain_sb[:, :], mat_ps, mask[:, :], ALU.mult).then_inc(chain_in, 1)
                elif n == 2:
                    dve.wait_ge(chain_out, CHAIN * q + 3)
                    dve.tensor_copy(chain_sb[:, :], mat_ps).then_inc(chain_in, 1)
                else:
                    dve.wait_ge(chain_out, CHAIN * q + 4)
                    dve.scalar_tensor_tensor(out=a_full[:, :], in0=mat_ps, scalar=rstd[:, 0:1], in1=ident[:, :],
                                             op0=ALU.mult, op1=ALU.add).then_inc(a_ready, 1)

            def macro_step(i, q, conv, attend):
                if known(i, 0):
                    steps[0] = 0
                last_round = known(i, MACROS - 1)
                norm = 1 if last_round else 0

                for tile in range(4):
                    work = work_of(i, tile, attend)
                    sums_at, windows_at, middle_at = places(work)
                    prepared = next_units(i, tile, last_round) if conv else []
                    t, slot = 2 * i + tile // 2, tile // 2
                    if known(q, 0) and known(i, 0) and tile == 0:
                        for j in range(sum(EARLY)):
                            x_statistics(q, j)

                    def sums():
                        if conv and tile % 2 == 1:
                            take_m2(q - 1, t, slot, i)
                        elif conv and not known(t, 0):
                            finish_rows(q - 1, t - 1, 1 - slot, 1)

                    def convolution_part(n):
                        if n == sums_at:
                            sums()
                        for (ahead, unit), at in zip(prepared, windows_at):
                            if n == at and not (known(ahead, 0) and unit == M0):
                                window_lo(q - 1, ahead, unit)
                        if conv and n == middle_at and tile % 2 == 1:
                            finish_rows(q - 1, t, slot, 0)

                    for n, w in enumerate(work or [("rest",)]):
                        if w[0] != "attend":
                            convolution_part(n)
                        if w[0] == "stats":
                            j = w[1]
                            ins = x_statistics(q, j)
                            if j == TILES - 1:
                                settle(q, ins)
                        elif w[0] in ("gather", "mean", "variance"):
                            if last_round and w[0] == "variance":
                                window_lo(q, 0, M1)
                            group_norm(q, norm, w[0])
                        elif w[0] == "scale":
                            start_attention(q)
                        elif w == ("first", 0):
                            dve.wait_ge(start_set, q + 1)
                            running_max(q, 0, 0)
                            centre(q, 2, 0)
                        elif w == ("first", 1):
                            running_max(q, 1, 1)
                            key_lo(q, 2, 0)
                        elif w[0] == "attend":
                            j, k = w[1], w[2]
                            if more(j, 3):
                                centre(q, j + 3, (k + 3) % 2)
                            if more(j, 2):
                                running_max(q, j + 2, k + 2)
                            if more(j, 3):
                                key_lo(q, j + 3, (k + 3) % 2)
                            convolution_part(n)
                            add_gram(q, j, k)
                        elif w[0] == "chain":
                            if w[1] == 0 and not conv:
                                prepare_weights()
                            chain(q, w[1], sums)
                        elif w[0] == "project":
                            j = w[1]
                            dve.wait_ge(x1_ready, TILES * q + j + 1)
                            ins = dve.bn_stats(x1_stats[:, 6 * j:6 * j + 6], x1_chunk(j))
                            if j == TILES - 1:
                                settle(q, ins)
                                group_norm(q, 1, "gather")
                    if attend and isinstance(i, int) and not known(q, IMAGES - 1):
                        for j in early_statistics(i, tile):
                            x_statistics(q + 1, j)

            def transition(q, conv, attend):
                if attend:
                    dve.wait_ge(rstd_ready, 2 * q + 2)
                    for n, (unit, c0, c1) in enumerate(W_PIECES):
                        w = slice(c0 * CH, c1 * CH)
                        if n == 1:
                            centre_column = slice((KSIZE - 1) * CH, KSIZE * CH)
                            dve.scalar_tensor_tensor(out=wc_mid[:, M1, :], in0=wc_raw[:, M1, centre_column],
                                                     scalar=rstd[:, 1:2], in1=half_ident[:, :], op0=ALU.mult,
                                                     op1=ALU.subtract).then_inc(wc_mid_ready, 1)
                            dve.scalar_tensor_tensor(out=wc_mid[:, M2, :], in0=wc_raw[:, M2, centre_column],
                                                     scalar=rstd[:, 1:2], in1=half_ident[:, :], op0=ALU.mult,
                                                     op1=ALU.add).then_inc(wc_mid_ready, 1)
                        if n == NEXT_UNIT_AT:
                            window_lo(q, 0, M2)
                        if conv and n == NEXT_UNIT_AT:
                            finish_rows(q - 1, CTILES - 1, 1, 1)
                        if n == len(W_PIECES) - 1:
                            window_lo(q, 0, M0)
                        dve.wait_ge(wc_hi_ready, len(W_PIECES) * q + n + 1)
                        if c1 == KSIZE and unit in (M1, M2):
                            dve.wait_ge(wc_mid_ready, 2 * q + unit - M1 + 1)
                            dve.tensor_tensor(wc_lo[:, unit, w], wc_mid[:, unit, :], wc_hi[:, unit, w].bitcast(f32),
                                              ALU.subtract).then_inc(wc_lo_ready, 1)
                        else:
                            dve.scalar_tensor_tensor(out=wc_lo[:, unit, w], in0=wc_raw[:, unit, w], scalar=rstd[:, 1:2],
                                                     in1=wc_hi[:, unit, w].bitcast(f32), op0=ALU.mult,
                                                     op1=ALU.subtract).then_inc(wc_lo_ready, 1)
                    if conv:
                        dve.wait_ge(y_made, 2 * CTILES * q)
                    dve.tensor_copy(out_bias[:, :], x1_mean[:, :]).then_inc(out_bias_ready, 1)
                    assert steps[0] == DVE_STEPS, steps[0]
                elif conv:
                    finish_rows(q - 1, CTILES - 1, 1, 1)

            dve.wait_ge(constants_set, 4)
            dve.memset(gram[:, :], 0.0).then_inc(gram_added, 1)
            image_steps(dve, macro_step, transition)

        @block.gpsimd
        def _(pool):
            pool.memset(win_hi[:, :, :, :].bitcast(f32), 0.0).then_inc(constants_set, 1)
            pool.memset(win_lo[:, :, :, :].bitcast(f32), 0.0).then_inc(constants_set, 1)
            pool.memset(xt[:, :, :, 0:ONES], 1.0).then_inc(constants_set, 1)
            pool.memset(minus_half[:, :], -0.5).then_inc(constants_set, 1)
            pool.wait_ge(constants_set, 4)

            def rstd_of(q, norm):
                pool.wait_ge(var_eps_ready, 2 * q + norm + 1)
                pool.tensor_tensor(rstd[:, norm:norm + 1], var_eps[:, norm:norm + 1], minus_half[:, :],
                                   ALU.pow).then_inc(rstd_ready, 1)

            def make_rows(p, t, unit, fresh=False):
                if not fresh and unit in (M1, M0):
                    pool.wait_ge(win_lo_ready, UNITS * (CTILES * p + t - 1) + unit + 2)
                dst = t_rows[:, unit, :, :]
                here = row_pairs(t * CT)
                if unit == M1:
                    pool.tensor_tensor(dst, here[:, 1], here[:, 0], ALU.subtract).then_inc(rows_made, 1)
                elif unit == M2:
                    pool.tensor_tensor(dst, here[:, 0], here[:, 1], ALU.add).then_inc(rows_made, 1)
                elif unit == M0 and known(t, 0):
                    pool.tensor_scalar(dst[:, 0, :], here[:, 1, 0], -1.0, x1_mean[:, 0:1], ALU.mult, ALU.add)
                    pool.tensor_tensor(dst[:, 1:, :], row_pairs(WIDTH, PAIRS - 1)[:, 0], here[:, 1, 1:],
                                       ALU.subtract).then_inc(rows_made, 1)
                elif unit == M0:
                    pool.tensor_tensor(dst, row_pairs(t * CT - WIDTH)[:, 0], here[:, 1], ALU.subtract).then_inc(rows_made, 1)
                elif known(t, CTILES - 1):
                    pool.tensor_scalar(dst[:, PAIRS - 1, :], here[:, 0, PAIRS - 1], -1.0, x1_mean[:, 0:1], ALU.mult, ALU.add)
                    pool.tensor_tensor(dst[:, 0:PAIRS - 1, :], here[:, 0, 1:], here[:, 0, 0:PAIRS - 1],
                                       ALU.subtract).then_inc(rows_made, 1)
                else:
                    pool.tensor_tensor(dst, row_pairs(t * CT + 2 * WIDTH)[:, 0], here[:, 0],
                                       ALU.subtract).then_inc(rows_made, 1)

            def macro_step(i, q, conv, attend):
                for tile in range(4):
                    if conv:
                        for t, unit in next_units(i, tile, known(i, MACROS - 1)):
                            if not (known(t, 0) and unit == M0):
                                make_rows(q - 1, t, unit, fresh=known(t, 0))
                    for w in work_of(i, tile, attend):
                        if w[0] == "variance" and i < MACROS - 1:
                            rstd_of(q, 0)

            def transition(q, conv, attend):
                if attend:
                    pool.wait_ge(x1_ready, TILES * q + CT // CHUNK)
                    make_rows(q, 0, M1, fresh=not conv)
                    make_rows(q, 0, M2, fresh=not conv)
                    rstd_of(q, 1)
                    make_rows(q, 0, M0, fresh=True)

            image_steps(pool, macro_step, transition)


_ORDER = ["x", "w_key", "w_value", "w_query", "w_out", "b_out", "w_top", "w_middle", "w_bottom", "identity", "group_mean", "head_mask"]


def kernel(x, L0_conv_w_qkv, L0_conv_w_out, L0_conv_b_out, L1_conv_weight):
    import concourse.bacc as bacc
    from concourse.bass_utils import run_bass_kernel_spmd

    x = np.asarray(x)
    w_qkv = np.asarray(L0_conv_w_qkv)
    per_group = CH // GROUPS
    channel = np.arange(CH)
    w_rows = np.asarray(L1_conv_weight).reshape(KSIZE, KSIZE, CH, CH)[:, list(COLUMNS)].transpose(0, 3, 1, 2)
    w_rows = np.ascontiguousarray(w_rows).reshape(KSIZE, CH, KSIZE * CH)
    arrays = {
        "x": x.reshape(IMAGES, CH, PIXELS),
        "w_key": np.ascontiguousarray(w_qkv[CH:2 * CH].T),
        "w_value": np.ascontiguousarray(w_qkv[2 * CH:3 * CH].T),
        "w_query": np.ascontiguousarray(w_qkv[0:CH]),
        "w_out": np.ascontiguousarray(np.asarray(L0_conv_w_out).T),
        "b_out": np.asarray(L0_conv_b_out).reshape(CH, 1),
        "w_top": w_rows[0], "w_middle": w_rows[1], "w_bottom": w_rows[2],
        "identity": np.eye(CH, dtype=np.float32),
        "group_mean": ((channel[:, None] // per_group == channel[None, :] // per_group) / per_group).astype(np.float32),
        "head_mask": (channel[:, None] // (CH // HEADS) == channel[None, :] // (CH // HEADS)).astype(np.float32),
    }
    nc = bacc.Bacc("TRN2", target_bir_lowering=False, num_devices=1, dynamic_dma_scratch_size=2048)
    args = [nc.dram_tensor(f"in_{n}", arrays[n].shape, mybir.dt.float32, kind="ExternalInput").ap() for n in _ORDER]
    args.append(nc.dram_tensor("out", (IMAGES, CH, PIXELS), mybir.dt.float32, kind="ExternalOutput").ap())
    build(nc, *args)
    result = run_bass_kernel_spmd(nc, [{f"in_{n}": arrays[n] for n in _ORDER}], core_ids=[0])
    return result.results[0]["out"].reshape(x.shape)
```
